# Optimizing a Trainium2 kernel written in Bass

```python
import numpy as np
import jax
import jax.numpy as jnp

def _softmax(x, axis=-1):
    return jax.nn.softmax(x, axis=axis)

def _gelu(x):
    return jax.nn.gelu(x, approximate=True)

def _silu(x):
    return jax.nn.silu(x)

def _sigmoid(x):
    return jax.nn.sigmoid(x)

def _layernorm(x, axis=-1, eps=1e-05):
    m = jnp.mean(x, axis=axis, keepdims=True)
    v = jnp.var(x, axis=axis, keepdims=True)
    return (x - m) / jnp.sqrt(v + eps)

def _scatter_add(tgt, idx, src, axis=0):
    return tgt.at[idx].add(src)

def _segment_sum(src, seg, n):
    return jax.ops.segment_sum(src, seg, n)
kernel_name = 'mk_adaln_ffn_d2_seqx_r8_da0e74'

def setup_inputs(seed: int=0):
    np.random.seed(seed)
    _w = jnp.asarray

    def _rec_inputs():
        import jax
        import jax.numpy as jnp
        _rk = jax.random.key(seed)
        x = 0.5 + 0.2886 * jax.random.normal(jax.random.fold_in(_rk, 1), (128, 32, 128), jnp.float32)
        _lenS = 32 - jax.random.randint(jax.random.fold_in(_rk, 7), (128,), 0, max(1, 32 // 4) + 1, jnp.int32)
        _lenS2 = 32 - jax.random.randint(jax.random.fold_in(_rk, 8), (128,), 0, max(1, 32 // 4) + 1, jnp.int32)
        fside_BxS_0 = jax.random.uniform(jax.random.fold_in(_rk, 11), (128, 32), jnp.float32, 0.0, 0.999994)
        cond_1024 = jax.random.uniform(jax.random.fold_in(_rk, 12), (128, 128), jnp.float32, 0.0, 0.999943)
        return (x, fside_BxS_0, cond_1024)
    x, fside_BxS_0, cond_1024 = _rec_inputs()

    def _L0_cond_setup():
        import jax, jax.numpy as jnp
        import numpy as np
        MU = 0.1
        TOL = 1e-09
        ITERS = 30
        EPS = 1e-12

        def _sinkhorn(M, r, c):
            K = jnp.exp(-M / MU)
            K = K / jnp.maximum(K.sum(axis=(-2, -1), keepdims=True), EPS)
            r_ = r[..., None]
            c_ = c[..., None]
            u0 = r_
            u_prev0 = jnp.ones_like(u0)
            v0 = jnp.zeros_like(c_)

            def step(carry, _):
                u, u_prev, v = carry
                diff = jnp.sqrt(jnp.sum((u - u_prev) ** 2, axis=-1))
                active = jnp.max(diff) > TOL
                v_new = c_ / jnp.maximum(jnp.einsum('bnm,bnk->bmk', K, u), EPS)
                u_new = r_ / jnp.maximum(jnp.einsum('bnm,bmk->bnk', K, v_new), EPS)
                u2 = jnp.where(active, u_new, u)
                v2 = jnp.where(active, v_new, v)
                up2 = jnp.where(active, u, u_prev)
                return ((u2, up2, v2), None)
            (u, _, v), _ = jax.lax.scan(step, (u0, u_prev0, v0), None, length=ITERS + 1)
            P = u * K * jnp.swapaxes(v, -2, -1)
            return P
        key = jax.random.key(seed)
        k1, k2, k3 = jax.random.split(key, 3)
        B, N, Nc = (32, 128, 128)
        M = jax.random.uniform(k1, (B, N, Nc), dtype=jnp.float32)
        r = jax.random.uniform(k2, (B, N), dtype=jnp.float32)
        c = jax.random.uniform(k3, (B, Nc), dtype=jnp.float32)
        return {'M': M, 'r': r, 'c': c}
    _L0_cond_all = _L0_cond_setup()
    _L0_cond_in = {k: v for k, v in _L0_cond_all.items() if k in ()}
    del _L0_cond_all

    def _L0_ffn_setup():
        import jax, jax.numpy as jnp
        import numpy as np
        B, S, H = (2, 128, 128)
        E, I, SI = (8, 64, 256)
        TOP_K, N_GROUP, TOPK_GROUP = (2, 2, 1)
        ROUTED_SCALE = 2.5

        def _route(x2d, gate_weight, gate_bias):
            T = x2d.shape[0]
            logits = x2d @ gate_weight.T
            scores = jax.nn.sigmoid(logits)
            sfc = scores + gate_bias[None, :]
            g = sfc.reshape(T, N_GROUP, E // N_GROUP)
            group_scores = jax.lax.top_k(g, 2)[0].sum(-1)
            _, gidx = jax.lax.top_k(group_scores, TOPK_GROUP)
            gmask = jnp.zeros((T, N_GROUP), sfc.dtype).at[jnp.arange(T)[:, None], gidx].set(1.0)
            smask = jnp.repeat(gmask, E // N_GROUP, axis=1)
            masked = jnp.where(smask > 0, sfc, 0.0)
            _, topk_idx = jax.lax.top_k(masked, TOP_K)
            topk_w = jnp.take_along_axis(scores, topk_idx, axis=1)
            topk_w = topk_w / (topk_w.sum(-1, keepdims=True) + 1e-20)
            topk_w = topk_w * ROUTED_SCALE
            return (topk_idx, topk_w)
        key = jax.random.key(seed)
        ks = jax.random.split(key, 7)

        def w(k, shape, sc=0.02):
            return jax.random.normal(k, shape, jnp.float32) * sc
        return {'hidden_states': jax.random.normal(ks[0], (B, S, H), jnp.float32), 'gate_weight': w(ks[1], (E, H)), 'gate_bias': w(ks[2], (E,), 0.01), 'up_weights': w(ks[3], (E, I, H)), 'down_weights': w(ks[4], (E, H, I)), 'shared_up_weight': w(ks[5], (SI, H)), 'shared_down_weight': w(ks[6], (H, SI))}
    _L0_ffn_all = _L0_ffn_setup()
    _L0_ffn_in = {k: v for k, v in _L0_ffn_all.items() if k in ('gate_weight', 'gate_bias', 'up_weights', 'down_weights', 'shared_up_weight', 'shared_down_weight')}
    del _L0_ffn_all

    def _L1_cond_setup():
        import jax, jax.numpy as jnp
        import numpy as np
        INPUT_DIM = 128
        HIDDEN_DIM = 128
        CHUNK_SIZE = 4

        def _linear_params(key, fan_in, fan_out):
            kw, kb = jax.random.split(key)
            bound = 1.0 / np.sqrt(fan_in)
            W = jax.random.uniform(kw, (fan_in, fan_out), jnp.float32, -bound, bound)
            b = jax.random.uniform(kb, (fan_out,), jnp.float32, -bound, bound)
            return (W, b)

        def _gru_forward(x, h0, Wz, bz, Wr, br, Wh, bh, Wp, bp):
            B, T, D = x.shape
            t = jnp.arange(T)
            do_prop = ((t + 1) % CHUNK_SIZE == 0) & (t < T - 1)
            xs = jnp.transpose(x, (1, 0, 2))

            def step(h, inp):
                x_t, prop = inp
                comb = jnp.concatenate([x_t, h], axis=-1)
                z = jax.nn.sigmoid(comb @ Wz + bz)
                r = jax.nn.sigmoid(comb @ Wr + br)
                comb2 = jnp.concatenate([x_t, r * h], axis=-1)
                h_cand = jnp.tanh(comb2 @ Wh + bh)
                h_new = (1.0 - z) * h + z * h_cand
                h_next = jnp.where(prop, jnp.tanh(h_new @ Wp + bp), h_new)
                return (h_next, h_new)
            _, ys = jax.lax.scan(step, h0, (xs, do_prop))
            return jnp.transpose(ys, (1, 0, 2))
        key = jax.random.key(seed)
        ks = jax.random.split(key, 6)
        x = jax.random.normal(ks[0], (64, 64, INPUT_DIM), jnp.float32)
        h0 = jax.random.normal(ks[1], (64, HIDDEN_DIM), jnp.float32)
        Wz, bz = _linear_params(ks[2], INPUT_DIM + HIDDEN_DIM, HIDDEN_DIM)
        Wr, br = _linear_params(ks[3], INPUT_DIM + HIDDEN_DIM, HIDDEN_DIM)
        Wh, bh = _linear_params(ks[4], INPUT_DIM + HIDDEN_DIM, HIDDEN_DIM)
        Wp, bp = _linear_params(ks[5], HIDDEN_DIM, HIDDEN_DIM)
        return {'x': x, 'h0': h0, 'Wz': Wz, 'bz': bz, 'Wr': Wr, 'br': br, 'Wh': Wh, 'bh': bh, 'Wp': Wp, 'bp': bp}
    _L1_cond_all = _L1_cond_setup()
    _L1_cond_in = {k: v for k, v in _L1_cond_all.items() if k in ('Wz', 'bz', 'Wr', 'br', 'Wh', 'bh', 'Wp', 'bp')}
    del _L1_cond_all

    def _L1_ffn_setup():
        import jax, jax.numpy as jnp
        import numpy as np
        B, N, D, H, E = (4, 128, 128, 16, 8)
        DK = D // H
        HID = 4 * D
        EPS = 1e-05

        def _layernorm(x, w, b):
            m = jnp.mean(x, axis=-1, keepdims=True)
            v = jnp.mean(jnp.square(x - m), axis=-1, keepdims=True)
            return (x - m) * jax.lax.rsqrt(v + EPS) * w + b

        def _msa(x, w_qkv, w_proj):
            b, n, d = x.shape
            qkv = (x @ w_qkv).reshape(b, n, 3, H, DK)
            q = qkv[:, :, 0].transpose(0, 2, 1, 3)
            k = qkv[:, :, 1].transpose(0, 2, 1, 3)
            v = qkv[:, :, 2].transpose(0, 2, 1, 3)
            attn = jnp.einsum('bhnd,bhmd->bhnm', q, k) * (1.0 / np.sqrt(DK))
            attn = jax.nn.softmax(attn, axis=-1)
            y = jnp.einsum('bhnm,bhmd->bhnd', attn, v)
            y = y.transpose(0, 2, 1, 3).reshape(b, n, d)
            return y @ w_proj

        def _moe_mlp(x, gate_w, gate_b, w1, w2):
            b, n, d = x.shape
            xf = x.reshape(b * n, d)
            logits = xf @ gate_w + gate_b
            one_hot = jax.nn.one_hot(jnp.argmax(logits, axis=-1), E, dtype=xf.dtype)
            h = jax.nn.gelu(jnp.einsum('td,edh->teh', xf, w1), approximate=True)
            y = jnp.einsum('teh,ehd->ted', h, w2)
            out = jnp.einsum('te,ted->td', one_hot, y)
            return out.reshape(b, n, d)
        key = jax.random.key(seed)
        ks = jax.random.split(key, 8)
        s = 0.02
        return {'x': jax.random.normal(ks[0], (B, N, D), jnp.float32), 'ln1_w': jnp.ones((D,), jnp.float32), 'ln1_b': jnp.zeros((D,), jnp.float32), 'w_qkv': jax.random.normal(ks[1], (D, 3 * D), jnp.float32) * s, 'w_proj': jax.random.normal(ks[2], (D, D), jnp.float32) * s, 'ln2_w': jnp.ones((D,), jnp.float32), 'ln2_b': jnp.zeros((D,), jnp.float32), 'gate_w': jax.random.normal(ks[3], (D, E), jnp.float32) * s, 'gate_b': jnp.zeros((E,), jnp.float32), 'w1': jax.random.normal(ks[4], (E, D, HID), jnp.float32) * s, 'w2': jax.random.normal(ks[5], (E, HID, D), jnp.float32) * s}
    _L1_ffn_all = _L1_ffn_setup()
    _L1_ffn_in = {k: v for k, v in _L1_ffn_all.items() if k in ('ln1_w', 'ln1_b', 'w_qkv', 'w_proj', 'ln2_w', 'ln2_b', 'gate_w', 'gate_b', 'w1', 'w2')}
    del _L1_ffn_all
    return {'x': x, 'fside_BxS_0': fside_BxS_0, 'cond_1024': cond_1024, 'L0_ffn_gate_weight': _L0_ffn_in['gate_weight'], 'L0_ffn_gate_bias': _L0_ffn_in['gate_bias'], 'L0_ffn_up_weights': _L0_ffn_in['up_weights'], 'L0_ffn_down_weights': _L0_ffn_in['down_weights'], 'L0_ffn_shared_up_weight': _L0_ffn_in['shared_up_weight'], 'L0_ffn_shared_down_weight': _L0_ffn_in['shared_down_weight'], 'L1_cond_Wz': _L1_cond_in['Wz'], 'L1_cond_bz': _L1_cond_in['bz'], 'L1_cond_Wr': _L1_cond_in['Wr'], 'L1_cond_br': _L1_cond_in['br'], 'L1_cond_Wh': _L1_cond_in['Wh'], 'L1_cond_bh': _L1_cond_in['bh'], 'L1_cond_Wp': _L1_cond_in['Wp'], 'L1_cond_bp': _L1_cond_in['bp'], 'L1_ffn_ln1_w': _L1_ffn_in['ln1_w'], 'L1_ffn_ln1_b': _L1_ffn_in['ln1_b'], 'L1_ffn_w_qkv': _L1_ffn_in['w_qkv'], 'L1_ffn_w_proj': _L1_ffn_in['w_proj'], 'L1_ffn_ln2_w': _L1_ffn_in['ln2_w'], 'L1_ffn_ln2_b': _L1_ffn_in['ln2_b'], 'L1_ffn_gate_w': _L1_ffn_in['gate_w'], 'L1_ffn_gate_b': _L1_ffn_in['gate_b'], 'L1_ffn_w1': _L1_ffn_in['w1'], 'L1_ffn_w2': _L1_ffn_in['w2']}

def reference(x, fside_BxS_0, cond_1024, L0_ffn_gate_weight, L0_ffn_gate_bias, L0_ffn_up_weights, L0_ffn_down_weights, L0_ffn_shared_up_weight, L0_ffn_shared_down_weight, L1_cond_Wz, L1_cond_bz, L1_cond_Wr, L1_cond_br, L1_cond_Wh, L1_cond_bh, L1_cond_Wp, L1_cond_bp, L1_ffn_ln1_w, L1_ffn_ln1_b, L1_ffn_w_qkv, L1_ffn_w_proj, L1_ffn_ln2_w, L1_ffn_ln2_b, L1_ffn_gate_w, L1_ffn_gate_b, L1_ffn_w1, L1_ffn_w2):
    import jax
    import jax.numpy as jnp

    def _L0_cond_ref(M, r, c):
        import jax, jax.numpy as jnp
        import numpy as np
        MU = 0.1
        TOL = 1e-09
        ITERS = 30
        EPS = 1e-12

        def _sinkhorn(M, r, c):
            K = jnp.exp(-M / MU)
            K = K / jnp.maximum(K.sum(axis=(-2, -1), keepdims=True), EPS)
            r_ = r[..., None]
            c_ = c[..., None]
            u0 = r_
            u_prev0 = jnp.ones_like(u0)
            v0 = jnp.zeros_like(c_)

            def step(carry, _):
                u, u_prev, v = carry
                diff = jnp.sqrt(jnp.sum((u - u_prev) ** 2, axis=-1))
                active = jnp.max(diff) > TOL
                v_new = c_ / jnp.maximum(jnp.einsum('bnm,bnk->bmk', K, u), EPS)
                u_new = r_ / jnp.maximum(jnp.einsum('bnm,bmk->bnk', K, v_new), EPS)
                u2 = jnp.where(active, u_new, u)
                v2 = jnp.where(active, v_new, v)
                up2 = jnp.where(active, u, u_prev)
                return ((u2, up2, v2), None)
            (u, _, v), _ = jax.lax.scan(step, (u0, u_prev0, v0), None, length=ITERS + 1)
            P = u * K * jnp.swapaxes(v, -2, -1)
            return P
        return _sinkhorn(M, r, c)

    def _L0_ffn_ref(hidden_states, gate_weight, gate_bias, up_weights, down_weights, shared_up_weight, shared_down_weight):
        import jax, jax.numpy as jnp
        import numpy as np
        B, S, H = (2, 128, 128)
        E, I, SI = (8, 64, 256)
        TOP_K, N_GROUP, TOPK_GROUP = (2, 2, 1)
        ROUTED_SCALE = 2.5

        def _route(x2d, gate_weight, gate_bias):
            T = x2d.shape[0]
            logits = x2d @ gate_weight.T
            scores = jax.nn.sigmoid(logits)
            sfc = scores + gate_bias[None, :]
            g = sfc.reshape(T, N_GROUP, E // N_GROUP)
            group_scores = jax.lax.top_k(g, 2)[0].sum(-1)
            _, gidx = jax.lax.top_k(group_scores, TOPK_GROUP)
            gmask = jnp.zeros((T, N_GROUP), sfc.dtype).at[jnp.arange(T)[:, None], gidx].set(1.0)
            smask = jnp.repeat(gmask, E // N_GROUP, axis=1)
            masked = jnp.where(smask > 0, sfc, 0.0)
            _, topk_idx = jax.lax.top_k(masked, TOP_K)
            topk_w = jnp.take_along_axis(scores, topk_idx, axis=1)
            topk_w = topk_w / (topk_w.sum(-1, keepdims=True) + 1e-20)
            topk_w = topk_w * ROUTED_SCALE
            return (topk_idx, topk_w)
        Bv, Sv, Hv = hidden_states.shape
        x = hidden_states.reshape(-1, Hv)
        T = x.shape[0]
        topk_idx, topk_w = _route(x, gate_weight, gate_bias)
        cw = jnp.zeros((T, E), x.dtype).at[jnp.arange(T)[:, None], topk_idx].add(topk_w)
        h = jnp.einsum('th,eih->tei', x, up_weights)
        r = jnp.maximum(h, 0.0)
        r2 = r * r
        routed = jnp.einsum('tei,ehi,te->th', r2, down_weights, cw)
        sh = jnp.maximum(x @ shared_up_weight.T, 0.0)
        shared = sh * sh @ shared_down_weight.T
        return (routed + shared).reshape(Bv, Sv, Hv)

    def _L1_cond_ref(x, h0, Wz, bz, Wr, br, Wh, bh, Wp, bp):
        import jax, jax.numpy as jnp
        import numpy as np
        INPUT_DIM = 128
        HIDDEN_DIM = 128
        CHUNK_SIZE = 4

        def _linear_params(key, fan_in, fan_out):
            kw, kb = jax.random.split(key)
            bound = 1.0 / np.sqrt(fan_in)
            W = jax.random.uniform(kw, (fan_in, fan_out), jnp.float32, -bound, bound)
            b = jax.random.uniform(kb, (fan_out,), jnp.float32, -bound, bound)
            return (W, b)

        def _gru_forward(x, h0, Wz, bz, Wr, br, Wh, bh, Wp, bp):
            B, T, D = x.shape
            t = jnp.arange(T)
            do_prop = ((t + 1) % CHUNK_SIZE == 0) & (t < T - 1)
            xs = jnp.transpose(x, (1, 0, 2))

            def step(h, inp):
                x_t, prop = inp
                comb = jnp.concatenate([x_t, h], axis=-1)
                z = jax.nn.sigmoid(comb @ Wz + bz)
                r = jax.nn.sigmoid(comb @ Wr + br)
                comb2 = jnp.concatenate([x_t, r * h], axis=-1)
                h_cand = jnp.tanh(comb2 @ Wh + bh)
                h_new = (1.0 - z) * h + z * h_cand
                h_next = jnp.where(prop, jnp.tanh(h_new @ Wp + bp), h_new)
                return (h_next, h_new)
            _, ys = jax.lax.scan(step, h0, (xs, do_prop))
            return jnp.transpose(ys, (1, 0, 2))
        return _gru_forward(x, h0, Wz, bz, Wr, br, Wh, bh, Wp, bp)

    def _L1_ffn_ref(x, ln1_w, ln1_b, w_qkv, w_proj, ln2_w, ln2_b, gate_w, gate_b, w1, w2):
        import jax, jax.numpy as jnp
        import numpy as np
        B, N, D, H, E = (4, 128, 128, 16, 8)
        DK = D // H
        HID = 4 * D
        EPS = 1e-05

        def _layernorm(x, w, b):
            m = jnp.mean(x, axis=-1, keepdims=True)
            v = jnp.mean(jnp.square(x - m), axis=-1, keepdims=True)
            return (x - m) * jax.lax.rsqrt(v + EPS) * w + b

        def _msa(x, w_qkv, w_proj):
            b, n, d = x.shape
            qkv = (x @ w_qkv).reshape(b, n, 3, H, DK)
            q = qkv[:, :, 0].transpose(0, 2, 1, 3)
            k = qkv[:, :, 1].transpose(0, 2, 1, 3)
            v = qkv[:, :, 2].transpose(0, 2, 1, 3)
            attn = jnp.einsum('bhnd,bhmd->bhnm', q, k) * (1.0 / np.sqrt(DK))
            attn = jax.nn.softmax(attn, axis=-1)
            y = jnp.einsum('bhnm,bhmd->bhnd', attn, v)
            y = y.transpose(0, 2, 1, 3).reshape(b, n, d)
            return y @ w_proj

        def _moe_mlp(x, gate_w, gate_b, w1, w2):
            b, n, d = x.shape
            xf = x.reshape(b * n, d)
            logits = xf @ gate_w + gate_b
            one_hot = jax.nn.one_hot(jnp.argmax(logits, axis=-1), E, dtype=xf.dtype)
            h = jax.nn.gelu(jnp.einsum('td,edh->teh', xf, w1), approximate=True)
            y = jnp.einsum('teh,ehd->ted', h, w2)
            out = jnp.einsum('te,ted->td', one_hot, y)
            return out.reshape(b, n, d)
        x = x + _msa(_layernorm(x, ln1_w, ln1_b), w_qkv, w_proj)
        x = x + _moe_mlp(_layernorm(x, ln2_w, ln2_b), gate_w, gate_b, w1, w2)
        return x
    x = x + _L0_ffn_ref(_L0_cond_ref(x, fside_BxS_0, cond_1024), L0_ffn_gate_weight, L0_ffn_gate_bias, L0_ffn_up_weights, L0_ffn_down_weights, L0_ffn_shared_up_weight, L0_ffn_shared_down_weight)
    x = x + _L1_ffn_ref(_L1_cond_ref(x, cond_1024, L1_cond_Wz, L1_cond_bz, L1_cond_Wr, L1_cond_br, L1_cond_Wh, L1_cond_bh, L1_cond_Wp, L1_cond_bp), L1_ffn_ln1_w, L1_ffn_ln1_b, L1_ffn_w_qkv, L1_ffn_w_proj, L1_ffn_ln2_w, L1_ffn_ln2_b, L1_ffn_gate_w, L1_ffn_gate_b, L1_ffn_w1, L1_ffn_w2)
    return x

_drawn_inputs = setup_inputs


def setup_inputs(seed=0):
    import zlib

    import numpy as np

    out = dict(_drawn_inputs(seed))
    spreads = {'L1_ffn_ln1_w': (1.0, 0.2),
     'L1_ffn_ln1_b': (0.0, 0.383),
     'L1_ffn_ln2_w': (1.0, 0.2),
     'L1_ffn_ln2_b': (0.0, 0.1),
     'L1_ffn_gate_b': (0.0, 0.1)}
    factors = {'fside_BxS_0': 8.0,
     'L0_ffn_gate_weight': 8.0,
     'L0_ffn_gate_bias': 8.0,
     'L0_ffn_up_weights': 8.0,
     'L0_ffn_down_weights': 8.0,
     'L0_ffn_shared_up_weight': 8.0,
     'L0_ffn_shared_down_weight': 8.0,
     'L1_cond_bz': 4.953,
     'L1_cond_Wr': 4.269,
     'L1_cond_br': 29.322}
    for name, (base, spread) in spreads.items():
        noise = np.random.default_rng([zlib.crc32(name.encode()), seed]).standard_normal(out[name].shape)
        drawn = base * np.exp(spread * noise) if base else spread * noise
        out[name] = jnp.asarray(drawn.astype(out[name].dtype))
    for name, factor in factors.items():
        out[name] = (out[name] * factor).astype(out[name].dtype)
    return out
```

```python
import concourse.bass as bass
from concourse import mybir
from contextlib import ExitStack

F32 = mybir.dt.float32
BF16 = mybir.dt.bfloat16
I32 = mybir.dt.int32
ALU = mybir.AluOpType
ACT = mybir.ActivationFunctionType
AX = mybir.AxisListType

P = 128
B, N, D = 128, 32, 128
T = B * N
G = T // P
BG = P // N
MU, TOL, EPS, ITERS = 0.1, 1e-9, 1e-12, 31
HALF = G // 2
HB = HALF * BG


class Memory:

    def __init__(self, nc, ctx):
        self.nc, self.ctx = nc, ctx

    def sb(self, name, shape, dt=F32):
        return self.ctx.enter_context(self.nc.sbuf_tensor(name, shape, dt))

    def ps(self, name, shape, dt=F32):
        return self.ctx.enter_context(self.nc.psum_tensor(name, shape, dt))

    def sem(self, name):
        return self.ctx.enter_context(self.nc.semaphore(name))


class Chain:

    def __init__(self, eng, sem, start=0):
        self.eng, self.sem, self.n = eng, sem, start

    def step(self, ins):
        ins.then_inc(self.sem, 1)
        self.n = self.n + 1
        self.eng.wait_ge(self.sem, self.n)


def high_halves(t):
    return t[:].bitcast(BF16).rearrange("p k (m two) -> p k m two", two=2)[:, :, :, 1]


def constants(nc, mem, keep):
    ident = keep.sb("ident", [P, P])
    same_batch = keep.sb("same_batch", [P, P])
    own_batch = keep.sb("own_batch", [P, BG])
    ones = keep.sb("ones", [P, P])
    neg_tol = keep.sb("neg_tol", [P, 1])
    rounds = keep.sb("rounds", [1, ITERS])
    ident_b = keep.sb("ident_b", [P, P], BF16)
    made = mem.sem("const_made")
    with nc.Block() as block:

        @block.gpsimd
        def _(pool):
            g = nc.gpsimd
            c = Chain(pool, made)
            c.step(g.memset(ident[:], 0.0))
            c.step(g.affine_select(out=ident[:], in_=ident[:], compare_op=ALU.not_equal, fill=1.0,
                                   base=0, pattern=[[-1, P]], channel_multiplier=1))
            c.step(g.memset(ones[:], 1.0))
            c.step(g.memset(neg_tol[:], -TOL))
            c.step(g.iota(rounds[:], pattern=[[1, ITERS]], base=0, channel_multiplier=0,
                          allow_small_or_imprecise_dtypes=True))
            c.step(g.tensor_copy(ident_b[:], ident[:]))
            for t, width in ((same_batch, N), (own_batch, 1)):
                v = t[:].rearrange("p (b n) -> p b n", n=width)
                c.step(g.memset(t[:], 1.0))
                c.step(g.affine_select(out=v, in_=v, compare_op=ALU.is_ge, fill=0.0, base=0,
                                       pattern=[[-N, BG], [0, width]], channel_multiplier=1))
                c.step(g.affine_select(out=v, in_=v, compare_op=ALU.is_ge, fill=0.0, base=N - 1,
                                       pattern=[[N, BG], [0, width]], channel_multiplier=-1))
    return ident, ident_b, same_batch, own_batch, ones, neg_tol, rounds


def sinkhorn(nc, io, consts, K, KT, u_last, v_last):
    ident, ident_b, same_batch, own_batch, ones, neg_tol, rounds = consts
    with ExitStack() as ctx:
        mem = Memory(nc, ctx)
        kp = mem.sb("k_parts", [P, 3, T], BF16)
        ktp = mem.sb("kt_parts", [P, 3, T], BF16)
        rest = mem.sb("rest", [P, T])
        c_t = mem.sb("c_t", [P, B])
        r_t = mem.sb("r_t", [P, G])
        r_blk = mem.sb("r_blk", [P, G, BG])
        ksum = mem.sb("ksum", [P, G])
        ktsum = mem.sb("ktsum", [P, B])
        kinv = mem.sb("kinv", [P, G])
        ktinv = mem.sb("ktinv", [P, B])
        u3 = mem.sb("u3", [P, 3, B])
        v3 = mem.sb("v3", [P, 3, B])
        u_hist = mem.sb("u_hist", [P, ITERS + 2, B])
        v_hist = mem.sb("v_hist", [P, ITERS + 1, B])
        u_diff = mem.sb("u_diff", [P, B])
        over = mem.sb("over", [P, 2, B])
        still = mem.sb("still", [1, 2, ITERS])
        stop = mem.sb("stop", [1, 1])
        stop_i = mem.sb("stop_i", [1, 1], I32)
        moved = mem.sb("moved", [P, ITERS])
        tot = mem.sb("tot", [P, 2, HB])
        den = mem.sb("den", [P, 2, HB])
        inv = mem.sb("inv", [P, 2, HB])
        ps_v = [mem.ps(f"ps_v{h}", [P, 512]) for h in range(2)]
        ps_u = [mem.ps(f"ps_u{h}", [P, 512]) for h in range(2)]
        s = {n: mem.sem(n) for n in ("x_in", "xt_in", "cr_in", "k_exp", "kt_exp", "ksum_ready", "sums_mm",
                                     "k_scaled", "part1", "dve", "parts_ready", "v_mm", "u_mm", "v_ready", "u_ready",
                                     "v_kept", "u_kept", "u_read", "v_read", "diffed", "judged", "overs", "kdone")}
        xv = io["x"].rearrange("(g p) m -> p g m", p=P)
        Kv = K[:].rearrange("p (g m) -> p g m", m=D)
        KTv = KT[:].rearrange("p (b n) -> p b n", n=N)

        with nc.Block() as block:

            @block.sync
            def _(sp):
                sp.dma_start(KT[:], io["x_t"]).then_inc(s["xt_in"], 16)
                sp.dma_start(Kv, xv).then_inc(s["x_in"], 16)
                sp.dma_start(c_t[:], io["cond_t"]).then_inc(s["cr_in"], 16)
                sp.dma_start(r_t[:], io["r_t"]).then_inc(s["cr_in"], 16)

            @block.scalar
            def _(act):
                act.wait_ge(s["xt_in"], 16)
                nc.scalar.activation(KT[:], KT[:], ACT.Exp, scale=-1.0 / MU).then_inc(s["kt_exp"], 1)
                act.wait_ge(s["x_in"], 16)
                nc.scalar.activation(K[:], K[:], ACT.Exp, scale=-1.0 / MU).then_inc(s["k_exp"], 1)
                act.wait_ge(s["k_scaled"], 1)
                nc.scalar.copy(ktp[:, 0, :], KT[:]).then_inc(s["part1"], 1)
                act.wait_ge(s["k_scaled"], 2)
                nc.scalar.copy(kp[:, 0, :], K[:]).then_inc(s["part1"], 1)

            @block.tensor
            def _(pe):
                pe.wait_ge(s["ksum_ready"], 1)
                nc.tensor.matmul(ps_v[0][:, 0:B], ones[:], ktsum[:], start=True, stop=True).then_inc(s["sums_mm"], 1)
                pe.wait_ge(s["ksum_ready"], 2)
                nc.tensor.matmul(ps_v[1][:, 0:G], same_batch[:], ksum[:], start=True, stop=True).then_inc(s["sums_mm"], 1)

            @block.vector
            def _(dve):
                v = nc.vector
                c = Chain(dve, s["dve"])
                dve.wait_ge(s["kt_exp"], 1)
                v.tensor_reduce(ktsum[:], KTv, AX.X, ALU.add).then_inc(s["ksum_ready"], 1)
                dve.wait_ge(s["k_exp"], 1)
                v.tensor_reduce(ksum[:], Kv, AX.X, ALU.add).then_inc(s["ksum_ready"], 1)
                dve.wait_ge(s["sums_mm"], 1)
                c.step(v.tensor_scalar(ktinv[:], ps_v[0][:, 0:B], EPS, None, ALU.max))
                c.step(v.reciprocal(ktinv[:], ktinv[:]))
                v.tensor_tensor(KTv, KTv, ktinv[:, :, None].broadcast_to([P, B, N]), ALU.mult).then_inc(s["k_scaled"], 1)
                dve.wait_ge(s["sums_mm"], 2)
                c.step(v.tensor_scalar(kinv[:], ps_v[1][:, 0:G], EPS, None, ALU.max))
                c.step(v.reciprocal(kinv[:], kinv[:]))
                v.tensor_tensor(Kv, Kv, kinv[:, :, None].broadcast_to([P, G, D]), ALU.mult).then_inc(s["k_scaled"], 1)
                for n, (whole, parts) in enumerate(((KT, ktp), (K, kp))):
                    dve.wait_ge(s["k_scaled"], n + 1)
                    dve.wait_ge(s["part1"], n + 1)
                    c.step(v.tensor_tensor(rest[:], whole[:], parts[:, 0, :], ALU.subtract))
                    c.step(v.tensor_copy(parts[:, 1, :], rest[:]))
                    c.step(v.tensor_tensor(parts[:, 2, :], rest[:], parts[:, 1, :], ALU.subtract))
                dve.wait_ge(s["cr_in"], 32)
                c.step(v.tensor_tensor(r_blk[:], r_t[:, :, None].broadcast_to([P, G, BG]),
                                       own_batch[:, None, :].broadcast_to([P, G, BG]), ALU.mult))
                c.step(v.tensor_copy(u3[:, 0, :], r_blk[:].rearrange("p g b -> p (g b)")))
                c.step(v.tensor_tensor(u3[:, 1, :], u3[:, 0, :], high_halves(u3)[:, 0, :], ALU.subtract))
                c.step(v.tensor_tensor(u3[:, 2, :], u3[:, 1, :], high_halves(u3)[:, 1, :], ALU.subtract))
                c.step(v.tensor_copy(u_hist[:, 0, :].rearrange("p (g b) -> p g b", b=BG),
                                     own_batch[:, None, :].broadcast_to([P, G, BG])))
                c.step(v.tensor_copy(u_hist[:, 1, :], u3[:, 0, :]))
                c.step(v.memset(v_hist[:, 0, :], 0.0))

        ends = {}
        with nc.Block() as block:

            @block.tensor
            def _(pe):
                uh, vh = high_halves(u3), high_halves(v3)

                def products(out, parts, moving, h, done):
                    for g in range(HALF):
                        gg = h * HALF + g
                        for part in range(3):
                            last = nc.tensor.matmul(out[:, 12 * g:12 * g + 12], parts[:, part, gg * P:(gg + 1) * P],
                                                    moving[:, :, gg * BG:(gg + 1) * BG],
                                                    start=part == 0, stop=part == 2)
                    last.then_inc(done, 1)

                with nc.tensor.Fori(0, ITERS) as i:
                    for h in range(2):
                        pe.wait_ge(s["u_ready"], i * 2 + h + 1)
                        products(ps_v[h], kp, uh, h, s["v_mm"])
                    for h in range(2):
                        pe.wait_ge(s["v_ready"], i * 2 + h + 1)
                        products(ps_u[h], ktp, vh, h, s["u_mm"])

            @block.vector
            def _(dve):
                v = nc.vector
                uh, vh = high_halves(u3), high_halves(v3)
                dve.sem_inc(s["u_ready"], 2)

                def scaled(ps, h, num, out3, highs, chain, done):
                    cols = slice(h * HB, (h + 1) * HB)
                    chain.step(v.tensor_reduce(tot[:, h, :], ps[:, 0:12 * HALF].rearrange("p (g k b) -> p g b k", k=3, b=BG),
                                               AX.X, ALU.add))
                    chain.step(v.tensor_scalar(den[:, h, :], tot[:, h, :], EPS, None, ALU.max))
                    chain.step(v.reciprocal(inv[:, h, :], den[:, h, :]))
                    chain.step(v.tensor_tensor(out3[:, 0, cols], inv[:, h, :], num[:, cols], ALU.mult))
                    chain.step(v.tensor_tensor(out3[:, 1, cols], out3[:, 0, cols], highs[:, 0, cols], ALU.subtract))
                    v.tensor_tensor(out3[:, 2, cols], out3[:, 1, cols], highs[:, 1, cols], ALU.subtract).then_inc(done, 1)

                base = 17
                r_flat = r_blk[:].rearrange("p g b -> p (g b)")
                with nc.vector.Fori(0, ITERS) as i:
                    c = Chain(dve, s["dve"], i * 20 + base)
                    for h in range(2):
                        dve.wait_ge(s["v_mm"], i * 2 + h + 1)
                        dve.wait_ge(s["v_kept"], i * 2 + h + 1)
                        scaled(ps_v[h], h, c_t, v3, vh, c, s["v_ready"])
                    for h in range(2):
                        dve.wait_ge(s["u_mm"], i * 2 + h + 1)
                        dve.wait_ge(s["u_kept"], i * 2 + h + 1)
                        scaled(ps_u[h], h, r_flat, u3, uh, c, s["u_ready"])

            @block.gpsimd
            def _(pool):
                g = nc.gpsimd
                pool.sem_inc(s["v_kept"], 2)
                pool.sem_inc(s["u_kept"], 2)
                pool.sem_inc(s["u_read"], 1)
                with nc.gpsimd.Fori(0, ITERS) as i:
                    pool.wait_ge(s["u_kept"], i * 2 + 2)
                    pool.wait_ge(s["u_read"], i + 1)
                    g.tensor_tensor(u_diff[:], u_hist[:, i + 1, :], u_hist[:, i, :], ALU.subtract).then_inc(s["diffed"], 1)
                    for h in range(2):
                        cols = slice(h * HB, (h + 1) * HB)
                        pool.wait_ge(s["v_ready"], i * 2 + h + 1)
                        g.tensor_copy(v_hist[:, i + 1, cols], v3[:, 0, cols]).then_inc(s["v_kept"], 1)
                    for h in range(2):
                        cols = slice(h * HB, (h + 1) * HB)
                        pool.wait_ge(s["u_ready"], i * 2 + h + 3)
                        g.tensor_copy(u_hist[:, i + 2, cols], u3[:, 0, cols]).then_inc(s["u_kept"], 1)

            @block.scalar
            def _(act):
                with nc.scalar.Fori(0, ITERS) as i:
                    act.wait_ge(s["diffed"], i + 1)
                    nc.scalar.activation(over[:, 0, :], u_diff[:], ACT.Abs).then_inc(s["u_read"], 1)
                    act.wait_ge(s["u_read"], i + 2)
                    nc.scalar.activation(over[:, 1, :], over[:, 0, :], ACT.Relu, bias=neg_tol[:],
                                         accum_out=moved[:, bass.ds(i, 1)]).then_inc(s["judged"], 1)
                    act.wait_ge(s["judged"], i + 1)

        with nc.Block() as block:

            @block.tensor
            def _(pe):
                nc.tensor.matmul(ps_v[0][0:1, 0:ITERS], ones[:, 0:1], moved[:], start=True, stop=True).then_inc(s["overs"], 1)

            @block.vector
            def _(dve):
                v = nc.vector
                c = Chain(dve, s["kdone"])
                dve.wait_ge(s["overs"], 1)
                c.step(v.tensor_scalar(still[:, 0, :], ps_v[0][0:1, 0:ITERS], 0.0, float(2 * ITERS), ALU.is_gt, ALU.mult))
                c.step(v.tensor_tensor(still[:, 1, :], still[:, 0, :], rounds[:], ALU.add))
                c.step(v.tensor_reduce(stop[:], still[:, 1, :], AX.X, ALU.min))
                c.step(v.tensor_scalar(stop_i[:], stop[:], float(ITERS), None, ALU.min))
                k = v.value_load(stop_i[0:1, 0:1], min_val=0, max_val=ITERS)
                c.step(v.tensor_reduce(u_last[:], u_hist[:, k + 1, :].rearrange("p (g b) -> p g b", b=BG), AX.X, ALU.add))
                c.step(v.tensor_copy(v_last[:], v_hist[:, k, :]))


def plan_tokens(nc, io, consts, K, KT, u_last, v_last, cw_t):
    ident, ident_b = consts[0], consts[1]
    E, GE = 8, 4
    CH = 4
    with ExitStack() as ctx:
        mem = Memory(nc, ctx)
        gate_w = mem.sb("gate_w", [P, E])
        gate_b = mem.sb("gate_b", [P, E])
        prefer = mem.sb("prefer", [P, E])
        scores = mem.sb("scores", [P, G, E])
        biased = mem.sb("biased", [P, G, E])
        pair_hi = mem.sb("pair_hi", [P, 2 * G, 2])
        pair_lo = mem.sb("pair_lo", [P, 2 * G, 2])
        best = mem.sb("best", [P, 2 * G])
        second = mem.sb("second", [P, 2 * G])
        third = mem.sb("third", [P, 2 * G])
        gmask = mem.sb("gmask", [P, G, 2])
        eq = mem.sb("eq", [P, G, E])
        top = mem.sb("top", [P, G])
        hot = mem.sb("hot", [P, 2, G, E])
        cw = mem.sb("cw", [P, G, E])
        cw_left = mem.sb("cw_left", [P, G, E])
        cw_parts = mem.sb("cw_parts", [P, G, E, 3], BF16)
        ps_t = [mem.ps(f"ps_t{h}", [P, 512]) for h in range(2)]
        ps_l = mem.ps("ps_l", [P, G, E])
        ps_c = [mem.ps(f"ps_c{h}", [3 * E, 1024], BF16) for h in range(2)]
        gate_in, pref, scaled, t_mm, pt_ready, l_mm, scored, dve_s, split, c_mm, c_copied = (
            mem.sem(n) for n in ("gate_in", "pref", "scaled", "t_mm", "pt_ready", "l_mm", "scored", "rt_dve", "split",
                                 "c_mm", "c_copied"))
        with nc.Block() as block:

            @block.sync
            def _(sp):
                sp.dma_start(gate_w[:], io["gate_w0_t"]).then_inc(gate_in, 16)
                sp.dma_start(gate_b[:], io["gate_b0"].broadcast_to([P, E])).then_inc(gate_in, 16)

            @block.gpsimd
            def _(pool):
                nc.gpsimd.iota(prefer[:], pattern=[[-1, E]], base=E, channel_multiplier=0,
                               allow_small_or_imprecise_dtypes=True).then_inc(pref, 1)

            @block.tensor
            def _(pe):
                pe.wait_ge(gate_in, 32)
                for c in range(G // CH):
                    pe.wait_ge(scaled, c + 1)
                    if c >= 2:
                        pe.wait_ge(pt_ready, c - 1)
                    for g in range(CH):
                        gg = c * CH + g
                        last = nc.tensor.transpose(ps_t[c % 2][:, g * P:(g + 1) * P], K[:, gg * P:(gg + 1) * P], ident[:])
                    last.then_inc(t_mm, 1)
                for c in range(G // CH):
                    pe.wait_ge(pt_ready, c + 1)
                    for gg in range(c * CH, (c + 1) * CH):
                        last = nc.tensor.matmul(ps_l[:, gg, :], KT[:, gg * P:(gg + 1) * P], gate_w[:], start=True, stop=True)
                last.then_inc(l_mm, 1)
                pe.wait_ge(split, 1)
                for c in range(G // 8):
                    if c >= 2:
                        pe.wait_ge(c_copied, c - 1)
                    for g in range(8):
                        last = nc.tensor.transpose(ps_c[c % 2][:, g * P:(g + 1) * P],
                                                   cw_parts[:, c * 8 + g].rearrange("p e k -> p (e k)"), ident_b[:])
                    last.then_inc(c_mm, 1)

            @block.scalar
            def _(act):
                act.wait_ge(l_mm, 1)
                nc.scalar.activation(scores[:], ps_l[:], ACT.Sigmoid).then_inc(scored, 1)
                for c in range(G // 8):
                    act.wait_ge(c_mm, c + 1)
                    nc.scalar.copy(cw_t[:, c * 1024:(c + 1) * 1024], ps_c[c % 2][:]).then_inc(c_copied, 1)

            @block.vector
            def _(dve):
                v = nc.vector
                Kv = K[:].rearrange("p (g m) -> p g m", m=D)
                W = CH * P
                NB = CH * BG
                for c in range(G // CH + 1):
                    if c < G // CH:
                        v.tensor_tensor(Kv[:, c * CH:(c + 1) * CH, :], Kv[:, c * CH:(c + 1) * CH, :],
                                        u_last[:, c * CH:(c + 1) * CH, None].broadcast_to([P, CH, D]),
                                        ALU.mult).then_inc(scaled, 1)
                    if c >= 1:
                        b = c - 1
                        dve.wait_ge(t_mm, b + 1)
                        v.tensor_tensor(KT[:, b * W:(b + 1) * W].rearrange("p (b n) -> p b n", n=N),
                                        ps_t[b % 2][:].rearrange("p (b n) -> p b n", n=N),
                                        v_last[:, b * NB:(b + 1) * NB, None].broadcast_to([P, NB, N]),
                                        ALU.mult).then_inc(pt_ready, 1)
                c = Chain(dve, dve_s)
                dve.wait_ge(scored, 1)
                dve.wait_ge(pref, 1)
                dve.wait_ge(gate_in, 32)
                c.step(v.tensor_tensor(biased[:], scores[:], gate_b[:, None, :].broadcast_to([P, G, E]), ALU.add))
                quad = biased[:].rearrange("p g (q h w) -> p (g q) h w", q=2, w=2)
                c.step(v.tensor_tensor(pair_hi[:], quad[:, :, :, 0], quad[:, :, :, 1], ALU.max))
                c.step(v.tensor_tensor(pair_lo[:], quad[:, :, :, 0], quad[:, :, :, 1], ALU.min))
                c.step(v.tensor_tensor(best[:], pair_hi[:, :, 0], pair_hi[:, :, 1], ALU.max))
                c.step(v.tensor_tensor(second[:], pair_hi[:, :, 0], pair_hi[:, :, 1], ALU.min))
                c.step(v.tensor_tensor(third[:], pair_lo[:, :, 0], pair_lo[:, :, 1], ALU.max))
                c.step(v.tensor_tensor(second[:], second[:], third[:], ALU.max))
                c.step(v.tensor_tensor(best[:], best[:], second[:], ALU.add))
                gs = best[:].rearrange("p (g q) -> p g q", q=2)
                c.step(v.tensor_tensor(gmask[:, :, 0], gs[:, :, 0], gs[:, :, 1], ALU.is_ge))
                c.step(v.tensor_tensor(gmask[:, :, 1], gs[:, :, 0], gs[:, :, 1], ALU.is_lt))
                c.step(v.tensor_tensor(biased[:].rearrange("p g (q w) -> p (g q) w", q=2),
                                       biased[:].rearrange("p g (q w) -> p (g q) w", q=2),
                                       gmask[:].rearrange("p g q -> p (g q)")[:, :, None].broadcast_to([P, 2 * G, GE]), ALU.mult))
                for n in range(2):
                    c.step(v.tensor_reduce(top[:], biased[:], AX.X, ALU.max))
                    c.step(v.tensor_tensor(eq[:], biased[:], top[:, :, None].broadcast_to([P, G, E]), ALU.is_equal))
                    c.step(v.tensor_tensor(eq[:], eq[:], prefer[:, None, :].broadcast_to([P, G, E]), ALU.mult))
                    c.step(v.tensor_reduce(top[:], eq[:], AX.X, ALU.max))
                    c.step(v.tensor_tensor(hot[:, n], eq[:], top[:, :, None].broadcast_to([P, G, E]), ALU.is_equal))
                    if n == 0:
                        c.step(v.scalar_tensor_tensor(out=biased[:], in0=hot[:, 0], scalar=-1e30, in1=biased[:],
                                                      op0=ALU.mult, op1=ALU.add))
                c.step(v.tensor_tensor(hot[:, 0], hot[:, 0], hot[:, 1], ALU.add))
                c.step(v.tensor_tensor(cw[:], hot[:, 0], scores[:], ALU.mult))
                c.step(v.tensor_reduce(top[:], cw[:], AX.X, ALU.add))
                c.step(v.tensor_scalar(top[:], top[:], 1e-20, None, ALU.add))
                c.step(v.reciprocal(top[:], top[:]))
                c.step(v.tensor_tensor(cw[:], cw[:], top[:, :, None].broadcast_to([P, G, E]), ALU.mult))
                c.step(v.tensor_scalar(cw[:], cw[:], 2.5, None, ALU.mult))
                c.step(v.tensor_copy(cw_parts[:, :, :, 0], cw[:]))
                c.step(v.tensor_tensor(cw_left[:], cw[:], cw_parts[:, :, :, 0], ALU.subtract))
                c.step(v.tensor_copy(cw_parts[:, :, :, 1], cw_left[:]))
                v.tensor_tensor(cw_parts[:, :, :, 2], cw_left[:], cw_parts[:, :, :, 1], ALU.subtract).then_inc(split, 1)


def routed_ffn(nc, io, PT, cw_t, x1):
    J, JR = 6, 4
    W, NB = 512, 512 // N
    with ExitStack() as ctx:
        mem = Memory(nc, ctx)
        up = mem.sb("up0", [P, J * P])
        down = mem.sb("down0", [P, J, D])
        spread = mem.sb("spread", [24, JR, 2, 64], BF16)
        x_t2 = mem.sb("x_t2", [P, T])
        relu = mem.sb("relu", [P, 2, W])
        rc = mem.sb("rc", [P, W])
        gated = mem.sb("gated", [P, 2, W])
        ps_h = [mem.ps(f"ps_h{h}", [P, W]) for h in range(2)]
        ps_c = [mem.ps(f"ps_cw{h}", [P, W]) for h in range(2)]
        ps_y = [mem.ps(f"ps_y{h}", [P, W]) for h in range(2)]
        w_in, made, h_mm, c_mm, h_read, relu_ready, c_read, relu_read, g_ready, g_read, y_read = (
            mem.sem(n) for n in ("f_w_in", "f_made", "f_h_mm", "f_c_mm", "f_h_read", "f_relu_ready", "f_c_read",
                                 "f_relu_read", "f_g_ready", "f_g_read", "f_y_read"))
        with nc.Block() as block:

            @block.sync
            def _(sp):
                sp.dma_start(up[:], io["up0_t"]).then_inc(w_in, 16)
                sp.dma_start(down[:], io["down0_t"].rearrange("(j p) d -> p j d", p=P)).then_inc(w_in, 16)
                sp.dma_start(x_t2[:], io["x_t"]).then_inc(w_in, 16)

            @block.gpsimd
            def _(pool):
                g = nc.gpsimd
                c = Chain(pool, made)
                c.step(g.memset(spread[:], 1.0))
                c.step(g.affine_select(out=spread[:], in_=spread[:], compare_op=ALU.is_ge, fill=0.0, base=0,
                                       pattern=[[-6, JR], [-3, 2], [0, 64]], channel_multiplier=1))
                c.step(g.affine_select(out=spread[:], in_=spread[:], compare_op=ALU.is_ge, fill=0.0, base=2,
                                       pattern=[[6, JR], [3, 2], [0, 64]], channel_multiplier=-1))

            @block.tensor
            def _(pe):
                pe.wait_ge(w_in, 48)
                pe.wait_ge(made, 3)
                with nc.tensor.Fori(0, T // W // 2) as q:
                    for half in range(2):
                        tok = bass.ds(q * (2 * W) + half * W, W)
                        c = q * 2 + half
                        for j in range(J + 1):
                            if j < JR:
                                pe.wait_ge(c_read, c * JR + j + 1)
                            if j < J:
                                pe.wait_ge(h_read, c * J + j + 1)
                                nc.tensor.matmul(ps_h[j % 2][:], up[:, j * P:(j + 1) * P], PT[:, tok],
                                                 start=True, stop=True).then_inc(h_mm, 1)
                            if j < JR:
                                nc.tensor.matmul(ps_c[j % 2][:], spread[:, j].rearrange("p a b -> p (a b)"), cw_t[:, tok],
                                                 start=True, stop=True).then_inc(c_mm, 1)
                            if j >= 1:
                                i = j - 1
                                if i == 0:
                                    pe.wait_ge(y_read, c + 1)
                                pe.wait_ge(g_ready, c * J + i + 1)
                                nc.tensor.matmul(ps_y[half][:], down[:, i, :], gated[:, i % 2, :],
                                                 start=i == 0, stop=i == J - 1).then_inc(g_read, 1)

            @block.scalar
            def _(act):
                act.sem_inc(h_read, 2)
                with nc.scalar.Fori(0, T // W) as c:
                    for j in range(J):
                        act.wait_ge(h_mm, c * J + j + 1)
                        act.wait_ge(relu_read, c * J + j + 1)
                        nc.scalar.activation(relu[:, j % 2, :], ps_h[j % 2][:], ACT.Relu).then_inc(h_read, 1)

            @block.vector
            def _(dve):
                v = nc.vector
                dve.sem_inc(relu_read, 2)
                dve.sem_inc(c_read, 2)
                dve.sem_inc(g_read, 2)
                dve.sem_inc(y_read, 2)
                dve.wait_ge(w_in, 48)
                with nc.vector.Fori(0, T // W // 2) as q:
                    for half in range(2):
                        c = q * 2 + half
                        for j in range(J):
                            dve.wait_ge(h_read, c * J + j + 3)
                            other = relu[:, j % 2, :]
                            if j < JR:
                                dve.wait_ge(c_mm, c * JR + j + 1)
                                v.tensor_tensor(rc[:], relu[:, j % 2, :], ps_c[j % 2][:], ALU.mult).then_inc(c_read, 1)
                                dve.wait_ge(c_read, c * JR + j + 3)
                                other = rc[:]
                            dve.wait_ge(g_read, c * J + j + 1)
                            v.tensor_tensor(gated[:, j % 2, :], relu[:, j % 2, :], other, ALU.mult).then_inc(g_ready, 1)
                            dve.wait_ge(g_ready, c * J + j + 1)
                            dve.sem_inc(relu_read, 1)
                        dve.wait_ge(g_read, c * J + J + 2)
                        v.tensor_tensor(x1[:, :, bass.ds(q * (2 * NB) + half * NB, NB)].rearrange("p n b -> p b n"),
                                        ps_y[half][:].rearrange("p (b n) -> p b n", n=N),
                                        x_t2[:, bass.ds(q * (2 * W) + half * W, W)].rearrange("p (b n) -> p b n", n=N),
                                        ALU.add).then_inc(y_read, 1)


def gru(nc, io, x1, ys):
    STEPS = 4
    Z, R, C = range(3)
    with ExitStack() as ctx:
        mem = Memory(nc, ctx)
        wx = mem.sb("gru_wx", [P, 3, D])
        wh = mem.sb("gru_wh", [P, 3, D])
        wp = mem.sb("gru_wp", [P, D])
        bias = mem.sb("gru_b", [P, 4])
        h_in = mem.sb("h_in", [P, B])
        gate = mem.sb("gate", [P, 3, B])
        rh = mem.sb("rh", [P, B])
        zh = mem.sb("zh", [P, B])
        kept = mem.sb("kept", [P, B])
        fresh = mem.sb("fresh", [P, B])
        ps = [[mem.ps(f"ps_g{n}{k}", [P, B * 4]) for k in range(2)] for n in range(3)]
        ps_p = mem.ps("ps_prop", [P, 512])
        w_in, gates_mm, c_mm, p_mm, r_done, z_done, c_done, h_done, rh_done, y_done, own = (
            mem.sem(n) for n in ("g_w_in", "g_gates_mm", "g_c_mm", "g_p_mm", "g_r_done", "g_z_done", "g_c_done",
                                 "g_h_done", "g_rh_done", "g_y_done", "g_own"))
        with nc.Block() as block:

            @block.sync
            def _(sp):
                sp.dma_start(wx[:], io["gru_wx"].rearrange("(g p) d -> p g d", p=P)).then_inc(w_in, 16)
                sp.dma_start(wh[:], io["gru_wh"].rearrange("(g p) d -> p g d", p=P)).then_inc(w_in, 16)
                sp.dma_start(wp[:], io["gru_wp"]).then_inc(w_in, 16)
                sp.dma_start(bias[:], io["gru_b"]).then_inc(w_in, 16)
                sp.dma_start(h_in[:], io["cond_t"]).then_inc(w_in, 16)

            @block.tensor
            def _(pe):
                mm = nc.tensor.matmul

                def from_x(t, k):
                    for n in (R, Z, C):
                        mm(ps[n][k][:, 0:B], wx[:, n, :], x1[:, t, :], start=True, stop=False)

                def chunk(q, last_chunk):
                    for k in range(STEPS):
                        t = q * STEPS + k
                        if k == 0:
                            if last_chunk or not isinstance(q, int):
                                pe.wait_ge(h_done, q)
                            h = h_in[:]
                        else:
                            pe.wait_ge(y_done, t)
                            h = ys[:, t - 1, :]
                        mm(ps[R][k % 2][:, 0:B], wh[:, R, :], h, start=False, stop=True).then_inc(gates_mm, 1)
                        mm(ps[Z][k % 2][:, 0:B], wh[:, Z, :], h, start=False, stop=True).then_inc(gates_mm, 1)
                        if not (last_chunk and k == STEPS - 1):
                            from_x(t + 1, (k + 1) % 2)
                        pe.wait_ge(rh_done, t + 1)
                        mm(ps[C][k % 2][:, 0:B], wh[:, C, :], rh[:], start=False, stop=True).then_inc(c_mm, 1)
                    if not last_chunk:
                        pe.wait_ge(y_done, q * STEPS + STEPS)
                        mm(ps_p[:, 0:B], wp[:], ys[:, q * STEPS + STEPS - 1, :], start=True, stop=True).then_inc(p_mm, 1)

                pe.wait_ge(w_in, 80)
                from_x(0, 0)
                chunk(0, False)
                with nc.tensor.Fori(1, N // STEPS - 1) as q:
                    chunk(q, False)
                chunk(N // STEPS - 1, True)

            @block.scalar
            def _(act):
                fn = nc.scalar.activation

                def chunk(q, last_chunk):
                    for k in range(STEPS):
                        t = q * STEPS + k
                        act.wait_ge(gates_mm, t * 2 + 1)
                        fn(gate[:, R, :], ps[R][k % 2][:, 0:B], ACT.Sigmoid, bias=bias[:, R:R + 1]).then_inc(r_done, 1)
                        act.wait_ge(gates_mm, t * 2 + 2)
                        fn(gate[:, Z, :], ps[Z][k % 2][:, 0:B], ACT.Sigmoid, bias=bias[:, Z:Z + 1]).then_inc(z_done, 1)
                        act.wait_ge(c_mm, t + 1)
                        fn(gate[:, C, :], ps[C][k % 2][:, 0:B], ACT.Tanh, bias=bias[:, C:C + 1]).then_inc(c_done, 1)
                    if not last_chunk:
                        act.wait_ge(p_mm, q + 1)
                        fn(h_in[:], ps_p[:, 0:B], ACT.Tanh, bias=bias[:, 3:4]).then_inc(h_done, 1)

                act.wait_ge(w_in, 80)
                chunk(0, False)
                with nc.scalar.Fori(1, N // STEPS - 1) as q:
                    chunk(q, False)
                chunk(N // STEPS - 1, True)

            @block.vector
            def _(dve):
                tt = nc.vector.tensor_tensor

                def chunk(q, first):
                    for k in range(STEPS):
                        t = q * STEPS + k
                        c = Chain(dve, own, t * 3)
                        dve.wait_ge(r_done, t + 1)
                        if k == 0:
                            if not first:
                                dve.wait_ge(h_done, q)
                            h = h_in[:]
                        else:
                            dve.wait_ge(y_done, t)
                            h = ys[:, t - 1, :]
                        tt(rh[:], gate[:, R, :], h, ALU.mult).then_inc(rh_done, 1)
                        dve.wait_ge(z_done, t + 1)
                        c.step(tt(zh[:], gate[:, Z, :], h, ALU.mult))
                        c.step(tt(kept[:], h, zh[:], ALU.subtract))
                        dve.wait_ge(c_done, t + 1)
                        c.step(tt(fresh[:], gate[:, Z, :], gate[:, C, :], ALU.mult))
                        tt(ys[:, t, :], kept[:], fresh[:], ALU.add).then_inc(y_done, 1)

                dve.wait_ge(w_in, 80)
                chunk(0, True)
                with nc.vector.Fori(1, N // STEPS) as q:
                    chunk(q, False)


class NormStats:

    def __init__(self, mem, name):
        self.six = mem.sb(name + "_six", [P, N, 6])
        self.mean = mem.sb(name + "_mean", [P, N])
        self.var = mem.sb(name + "_var", [P, N])
        self.a = mem.sb(name + "_a", [P, N])
        self.root = mem.sb(name + "_root", [P, N])
        self.rstd = mem.sb(name + "_rstd", [P, N])

    def variance(self, v, c):
        s = self.six
        c.step(v.tensor_tensor(self.mean[:], s[:, :, 1], s[:, :, 4], ALU.add))
        c.step(v.tensor_tensor(self.a[:], s[:, :, 1], s[:, :, 4], ALU.subtract))
        c.step(v.tensor_tensor(self.a[:], self.a[:], self.a[:], ALU.mult))
        c.step(v.tensor_scalar(self.a[:], self.a[:], 0.25, LN_EPS, ALU.mult, ALU.add))
        c.step(v.tensor_tensor(self.var[:], s[:, :, 2], s[:, :, 5], ALU.add))
        c.step(v.tensor_scalar(self.mean[:], self.mean[:], 0.5, None, ALU.mult))
        c.step(v.scalar_tensor_tensor(out=self.var[:], in0=self.var[:], scalar=1.0 / D, in1=self.a[:],
                                      op0=ALU.mult, op1=ALU.add))

    def inverse_root(self, v, c):
        c.step(v.reciprocal(self.rstd[:], self.root[:]))
        c.step(v.tensor_tensor(self.a[:], self.rstd[:], self.rstd[:], ALU.mult))
        c.step(v.tensor_tensor(self.a[:], self.a[:], self.var[:], ALU.mult))
        c.step(v.tensor_scalar(self.a[:], self.a[:], -0.5, 1.5, ALU.mult, ALU.add))
        c.step(v.tensor_tensor(self.rstd[:], self.rstd[:], self.a[:], ALU.mult))


LN_EPS = 1e-5
TC = 4
CHUNKS = N // TC


def norm_first(nc, io, consts, ys, y_nat, xn_t):
    ident = consts[0]
    with ExitStack() as ctx:
        mem = Memory(nc, ctx)
        st = NormStats(mem, "ln1")
        wb = mem.sb("ln1_wb", [P, 2])
        xh = mem.sb("ln1_xh", [P, N, D])
        ps_n = [mem.ps(f"ps_n{k}", [P, TC * D]) for k in range(2)]
        ps_x = [mem.ps(f"ps_x{k}", [P, TC * B]) for k in range(2)]
        wb_in, y_mm, y_out, stats, own, rooted, xh_done, x_mm, x_out = (
            mem.sem("a_" + n) for n in ("wb_in", "y_mm", "y_out", "stats", "own", "rooted", "xh_done", "x_mm", "x_out"))
        with nc.Block() as block:

            @block.sync
            def _(sp):
                sp.dma_start(wb[:], io["ln1_wb"]).then_inc(wb_in, 16)

            @block.tensor
            def _(pe):
                for c in range(CHUNKS):
                    if c >= 2:
                        pe.wait_ge(y_out, c - 1)
                    for k in range(TC):
                        last = nc.tensor.transpose(ps_n[c % 2][:, k * D:(k + 1) * D], ys[:, c * TC + k, :], ident[:])
                    last.then_inc(y_mm, 1)
                for c in range(CHUNKS):
                    pe.wait_ge(xh_done, (c + 1) * TC)
                    if c >= 2:
                        pe.wait_ge(x_out, c - 1)
                    for k in range(TC):
                        last = nc.tensor.transpose(ps_x[c % 2][:, k * B:(k + 1) * B], xh[:, c * TC + k, :], ident[:])
                    last.then_inc(x_mm, 1)

            @block.scalar
            def _(act):
                with nc.scalar.Fori(0, CHUNKS // 2) as q:
                    for k in range(2):
                        act.wait_ge(y_mm, q * 2 + k + 1)
                        nc.scalar.copy(y_nat[:, bass.ds((q * 2 + k) * TC, TC), :],
                                       ps_n[k][:].rearrange("p (t d) -> p t d", d=D)).then_inc(y_out, 1)
                act.wait_ge(stats, 1)
                nc.scalar.activation(st.root[:], st.var[:], ACT.Sqrt).then_inc(rooted, 1)
                act.wait_ge(wb_in, 16)
                with nc.scalar.Fori(0, CHUNKS // 2) as q:
                    for k in range(2):
                        act.wait_ge(x_mm, q * 2 + k + 1)
                        nc.scalar.activation(xn_t[:, :, bass.ds((q * 2 + k) * TC, TC)].rearrange("p b t -> p t b"),
                                             ps_x[k][:].rearrange("p (t b) -> p t b", b=B),
                                             ACT.Identity, scale=wb[:, 0:1], bias=wb[:, 1:2]).then_inc(x_out, 1)

            @block.vector
            def _(dve):
                v = nc.vector
                with nc.vector.Fori(0, CHUNKS) as q:
                    dve.wait_ge(y_out, q + 1)
                    for k in range(TC):
                        last = v.bn_stats(st.six[:, q * TC + k, :], y_nat[:, q * TC + k, :])
                    last.then_inc(own, 1)
                c = Chain(dve, own, CHUNKS)
                dve.wait_ge(own, CHUNKS)
                st.variance(v, c)
                dve.sem_inc(stats, 1)
                dve.wait_ge(rooted, 1)
                st.inverse_root(v, c)
                for t in range(N):
                    v.tensor_scalar(xh[:, t, :], y_nat[:, t, :], st.mean[:, t:t + 1], st.rstd[:, t:t + 1],
                                    ALU.subtract, ALU.mult).then_inc(xh_done, 1)


def attention(nc, io, consts, xn_t, o_t):
    CB = 8
    NC = B // CB
    J, R, DK = 4, 4, 8
    CT = CB * N
    SCALE = 1.0 / float(DK) ** 0.5
    with ExitStack() as ctx:
        mem = Memory(nc, ctx)
        w_qkv = mem.sb("w_qkv", [P, 3, D])
        block_mask = mem.sb("block_mask", [P, J, R])
        head_mask = mem.sb("head_mask", [P, J])
        xs = mem.sb("xs", [P, 2, CB, N])
        qm = mem.sb("qm", [P, CB, J, N])
        ks = mem.sb("ks", [P, CB, N])
        vb = mem.sb("vb", [P, 2, CB, R, J, DK])
        most = mem.sb("most", [P, R, CB])
        total = mem.sb("total", [P, R, CB])
        shifted = mem.sb("shifted", [P, R, CB, N])
        expd = mem.sb("expd", [P, R, CB, N])
        probs = mem.sb("probs", [P, R, CB, N])
        probs_t = mem.sb("probs_t", [P, R, CB, N])
        ps_qk = mem.ps("ps_qk", [P, 2, CT])
        ps_v = mem.ps("ps_vv", [P, CB * 2, R, DK])
        w_v = w_qkv[:, 2, :].rearrange("p (r j d) -> p r j d", j=J, d=DK)
        ps_s = mem.ps("ps_ss", [P, R, 512])
        ps_o = mem.ps("ps_o", [P, 512])
        names = ("w_in", "masks", "xs_in", "qk_mm", "v_mm", "s_mm", "o_mm", "qk_out", "v_out", "o_out", "s_read",
                 "exp_done", "own", "p_done", "pt_done", "vb_clear")
        (w_in, masks, xs_in, qk_mm, v_mm, s_mm, o_mm, qk_out, v_out, o_out, s_read, exp_done, own, p_done,
         pt_done, vb_clear) = (mem.sem("t_" + n) for n in names)
        s_view = ps_s[:, :, 0:CT].rearrange("p r (b k) -> p r b k", k=N)
        with nc.Block() as block:

            @block.sync
            def _(sp):
                sp.dma_start(w_qkv[:].rearrange("p k d -> p (k d)"), io["w_qkv"]).then_inc(w_in, 16)

            @block.gpsimd
            def _(pool):
                g = nc.gpsimd
                g.memset(vb[:], 0.0).then_inc(vb_clear, 1)
                c = Chain(pool, masks)
                c.step(g.memset(block_mask[:], 1.0))
                c.step(g.affine_select(out=block_mask[:], in_=block_mask[:], compare_op=ALU.is_ge, fill=0.0, base=0,
                                       pattern=[[-DK, J], [-J * DK, R]], channel_multiplier=1))
                c.step(g.affine_select(out=block_mask[:], in_=block_mask[:], compare_op=ALU.is_ge, fill=0.0,
                                       base=DK - 1, pattern=[[DK, J], [J * DK, R]], channel_multiplier=-1))
                with nc.gpsimd.Fori(0, NC) as i:
                    pool.wait_ge(own, i * 2 + 3)
                    pool.wait_ge(pt_done, i + 1)
                    g.tensor_tensor(probs[:].rearrange("p r b k -> p (r b) k"), expd[:].rearrange("p r b k -> p (r b) k"),
                                    total[:].rearrange("p r b -> p (r b)")[:, :, None].broadcast_to([P, R * CB, N]),
                                    ALU.mult).then_inc(p_done, 1)

            @block.tensor
            def _(pe):
                mm = nc.tensor.matmul

                def project(c, k):
                    x = xs[:, k].rearrange("p b n -> p (b n)")
                    pe.wait_ge(xs_in, c + 1)
                    mm(ps_qk[:, 0, :], w_qkv[:, 0, :], x, start=True, stop=True)
                    mm(ps_qk[:, 1, :], w_qkv[:, 1, :], x, start=True, stop=True).then_inc(qk_mm, 1)
                    for b in range(CB):
                        for j in range(J):
                            last = mm(ps_v[32 * j:32 * j + 32, b].rearrange("p r d -> p (r d)"), xs[:, k, b, :],
                                      w_v[:, :, j, :], start=True, stop=True)
                    last.then_inc(v_mm, 1)

                def scores(c):
                    pe.wait_ge(s_read, c + 1)
                    for b in range(CB):
                        for r in range(R):
                            rows = slice(32 * r, 32 * r + 32)
                            last = mm(ps_s[:, r, b * N:(b + 1) * N], qm[rows, b].rearrange("p j n -> p (j n)"),
                                      ks[rows, b, :], start=True, stop=True)
                    last.then_inc(s_mm, 1)

                def mix(c, k):
                    pe.wait_ge(pt_done, c + 2)
                    pe.wait_ge(o_out, c + 1)
                    for b in range(CB):
                        for r in range(R):
                            last = mm(ps_o[32 * r:32 * r + 32, b * N:(b + 1) * N],
                                      vb[:, k, b, r].rearrange("p j d -> p (j d)"), probs_t[:, r, b, :],
                                      start=True, stop=True)
                    last.then_inc(o_mm, 1)

                pe.wait_ge(w_in, 16)
                project(0, 0)

                def body(c, k, more):
                    pe.wait_ge(qk_out, c + 1)
                    scores(c)
                    pe.wait_ge(v_out, c + 1)
                    if more:
                        project(c + 1, 1 - k)
                    mix(c, k)

                with nc.tensor.Fori(0, NC // 2 - 1) as i:
                    body(i * 2, 0, True)
                    body(i * 2 + 1, 1, True)
                body(NC - 2, 0, True)
                body(NC - 1, 1, False)

            @block.scalar
            def _(act):
                fn = nc.scalar.activation
                act.wait_ge(masks, 4)
                act.wait_ge(vb_clear, 1)

                def stage(c, k):
                    nc.scalar.copy(xs[:, k], xn_t[:, bass.ds(c * CB, CB), :]).then_inc(xs_in, 1)

                def heads_apart(c, k):
                    act.wait_ge(qk_mm, c + 1)
                    for j in range(J):
                        fn(qm[:, :, j, :], ps_qk[:, 0, :].rearrange("p (b n) -> p b n", n=N), ACT.Copy,
                           scale=head_mask[:, j:j + 1])
                    nc.scalar.copy(ks[:].rearrange("p b n -> p (b n)"), ps_qk[:, 1, :]).then_inc(qk_out, 1)
                    act.wait_ge(v_mm, c + 1)
                    for j in range(J):
                        rows = slice(32 * j, 32 * j + 32)
                        last = nc.scalar.copy(vb[rows, k, :, :, j, :].rearrange("p b r d -> p (b r) d"),
                                              ps_v[rows, 0:CB].rearrange("p b r d -> p (b r) d"))
                    last.then_inc(v_out, 1)

                stage(0, 0)
                stage(1, 1)
                heads_apart(0, 0)
                act.sem_inc(o_out, 1)

                def body(c, k, left):
                    act.wait_ge(own, c * 2 + 2)
                    fn(expd[:].rearrange("p r b k -> p (r b k)"), shifted[:].rearrange("p r b k -> p (r b k)"),
                       ACT.Exp, scale=SCALE).then_inc(exp_done, 1)
                    if left >= 1:
                        if left >= 2:
                            act.wait_ge(v_mm, c + 1)
                            stage(c + 2, k)
                        heads_apart(c + 1, 1 - k)
                    act.wait_ge(o_mm, c + 1)
                    nc.scalar.copy(o_t[:, :, bass.ds(c * CB, CB)].rearrange("p n b -> p b n"),
                                   ps_o[:, 0:CT].rearrange("p (b n) -> p b n", n=N)).then_inc(o_out, 1)

                with nc.scalar.Fori(0, NC // 2 - 1) as i:
                    body(i * 2, 0, 2)
                    body(i * 2 + 1, 1, 2)
                body(NC - 2, 0, 1)
                body(NC - 1, 1, 0)

            @block.vector
            def _(dve):
                v = nc.vector
                dve.wait_ge(masks, 3)
                v.tensor_reduce(head_mask[:], block_mask[:], AX.X, ALU.add).then_inc(masks, 1)
                dve.sem_inc(s_read, 1)
                dve.sem_inc(own, 1)
                dve.sem_inc(pt_done, 1)
                dve.sem_inc(exp_done, 1)
                with nc.vector.Fori(0, NC) as i:
                    dve.wait_ge(s_mm, i + 1)
                    v.tensor_reduce(most[:].rearrange("p r b -> p r b"), s_view, AX.X, ALU.max).then_inc(masks, 1)
                    dve.wait_ge(masks, i + 5)
                    dve.wait_ge(exp_done, i + 1)
                    v.tensor_tensor(shifted[:], s_view, most[:, :, :, None].broadcast_to([P, R, CB, N]),
                                    ALU.subtract).then_inc(s_read, 1)
                    dve.wait_ge(s_read, i + 2)
                    dve.sem_inc(own, 1)
                    dve.wait_ge(exp_done, i + 2)
                    v.tensor_reduce(total[:], expd[:], AX.X, ALU.add).then_inc(w_in, 1)
                    dve.wait_ge(w_in, i + 17)
                    v.reciprocal(total[:], total[:]).then_inc(own, 1)
                    dve.wait_ge(p_done, i + 1)
                    v.transpose(probs_t[:].rearrange("p r b k -> p (r b k)"),
                                probs[:].rearrange("p r b k -> p (r b k)")).then_inc(pt_done, 1)


E_MOE, HID = 8, 4 * D
TILES = T // P + E_MOE - 1
SLOTS = TILES * P


def project_and_route(nc, io, consts, o_t, x2, xh, slot_i, expert_i, ln2_wb):
    ident, ones = consts[0], consts[4]
    E = E_MOE
    with ExitStack() as ctx:
        mem = Memory(nc, ctx)
        st = NormStats(mem, "ln2")
        w_proj = mem.sb("w_proj", [P, D])
        gate_w = mem.sb("gate_w1", [P, E])
        gate_b = mem.sb("gate_b1", [P, E])
        prefer = mem.sb("prefer1", [P, E])
        before = mem.sb("before", [P, P])
        tile_no = mem.sb("tile_no", [P, TILES])
        restart = mem.sb("restart", [P, E, N])
        xn = mem.sb("xn2", [P, 2, TC * B])
        logits = mem.sb("logits1", [P, N, E])
        top = mem.sb("top1", [P, N])
        eq = mem.sb("eq1", [P, N, E])
        hot = mem.sb("hot1", [P, N, E])
        count = mem.sb("count1", [P, E, N])
        seen = mem.sb("seen1", [P, E, N])
        tiles = mem.sb("tiles1", [P, E])
        tiles_i = mem.sb("tiles_i", [P, E], I32)
        tile_end = mem.sb("tile_end", [P, E])
        first_slot = mem.sb("first_slot", [P, E])
        past = mem.sb("past", [P, TILES, E - 1])
        expert = mem.sb("expert1", [P, TILES])
        ps_p = [mem.ps(f"ps_pr{k}", [P, TC * D]) for k in range(2)]
        ps_x = [mem.ps(f"ps_xt{k}", [P, TC * B]) for k in range(2)]
        ps_l = mem.ps("ps_lg", [P, N, E])
        ps_r = mem.ps("ps_rank", [P, N, E])
        ps_c = mem.ps("ps_count", [P, N, E])
        names = ("w_in", "made", "p_mm", "x2_done", "stats", "own", "rooted", "xh_done", "x_mm", "xn_out", "l_mm",
                 "hot_done", "r_mm")
        w_in, made, p_mm, x2_done, stats, own, rooted, xh_done, x_mm, xn_out, l_mm, hot_done, r_mm = (
            mem.sem("r_" + n) for n in names)
        with nc.Block() as block:

            @block.sync
            def _(sp):
                sp.dma_start(w_proj[:], io["w_proj"]).then_inc(w_in, 16)
                sp.dma_start(gate_w[:], io["gate_w1"]).then_inc(w_in, 16)
                sp.dma_start(gate_b[:], io["gate_b1"].broadcast_to([P, E])).then_inc(w_in, 16)
                sp.dma_start(ln2_wb[:], io["ln2_wb"]).then_inc(w_in, 16)

            @block.gpsimd
            def _(pool):
                g = nc.gpsimd
                c = Chain(pool, made)
                c.step(g.iota(prefer[:], pattern=[[-1, E]], base=E, channel_multiplier=0,
                              allow_small_or_imprecise_dtypes=True))
                c.step(g.iota(tile_no[:], pattern=[[1, TILES]], base=0, channel_multiplier=0,
                              allow_small_or_imprecise_dtypes=True))
                c.step(g.memset(before[:], 1.0))
                c.step(g.affine_select(out=before[:], in_=before[:], compare_op=ALU.is_ge, fill=0.0, base=-1,
                                       pattern=[[1, P]], channel_multiplier=-1))
                c.step(g.memset(restart[:], 1.0))
                c.step(g.memset(restart[:, :, 0], 0.0))

            @block.tensor
            def _(pe):
                mm = nc.tensor.matmul
                pe.wait_ge(w_in, 64)
                for c in range(CHUNKS):
                    if c >= 2:
                        pe.wait_ge(x2_done, c - 1)
                    for k in range(TC):
                        last = mm(ps_p[c % 2][:, k * D:(k + 1) * D], o_t[:, c * TC + k, :], w_proj[:], start=True, stop=True)
                    last.then_inc(p_mm, 1)
                for c in range(CHUNKS + 1):
                    if c < CHUNKS:
                        pe.wait_ge(xh_done, (c + 1) * TC)
                        if c >= 2:
                            pe.wait_ge(xn_out, c - 1)
                        for k in range(TC):
                            last = nc.tensor.transpose(ps_x[c % 2][:, k * B:(k + 1) * B], xh[:, c * TC + k, :], ident[:])
                        last.then_inc(x_mm, 1)
                    if c >= 1:
                        pe.wait_ge(xn_out, c)
                        for k in range(TC):
                            last = mm(ps_l[:, (c - 1) * TC + k, :], xn[:, (c - 1) % 2, k * B:(k + 1) * B], gate_w[:],
                                      start=True, stop=True)
                        last.then_inc(l_mm, 1)
                pe.wait_ge(hot_done, 1)
                pe.wait_ge(made, 6)
                hots = hot[:].rearrange("p t e -> p (t e)")
                mm(ps_r[:].rearrange("p t e -> p (t e)"), before[:], hots, start=True, stop=True).then_inc(r_mm, 1)
                mm(ps_c[:].rearrange("p t e -> p (t e)"), ones[:], hots, start=True, stop=True).then_inc(r_mm, 1)

            @block.scalar
            def _(act):
                act.wait_ge(stats, 1)
                nc.scalar.activation(st.root[:], st.var[:], ACT.Sqrt).then_inc(rooted, 1)
                act.wait_ge(w_in, 64)
                for c in range(CHUNKS):
                    act.wait_ge(x_mm, c + 1)
                    if c >= 2:
                        act.wait_ge(l_mm, c - 1)
                    nc.scalar.activation(xn[:, c % 2, :], ps_x[c % 2][:], ACT.Identity, scale=ln2_wb[:, 0:1],
                                         bias=ln2_wb[:, 1:2]).then_inc(xn_out, 1)

            @block.vector
            def _(dve):
                v = nc.vector
                with nc.vector.Fori(0, CHUNKS // 2) as q:
                    for h in range(2):
                        dve.wait_ge(p_mm, q * 2 + h + 1)
                        here = x2[:, bass.ds((q * 2 + h) * TC, TC), :]
                        v.tensor_tensor(here, ps_p[h][:].rearrange("p (t d) -> p t d", d=D), here, ALU.add).then_inc(x2_done, 1)
                        dve.wait_ge(x2_done, q * 2 + h + 1)
                        for k in range(TC):
                            t = (q * 2 + h) * TC + k
                            last = v.bn_stats(st.six[:, t, :], x2[:, t, :])
                        last.then_inc(own, 1)
                c = Chain(dve, own, CHUNKS)
                dve.wait_ge(own, CHUNKS)
                st.variance(v, c)
                dve.sem_inc(stats, 1)
                dve.wait_ge(rooted, 1)
                st.inverse_root(v, c)
                for t in range(N):
                    v.tensor_scalar(xh[:, t, :], x2[:, t, :], st.mean[:, t:t + 1], st.rstd[:, t:t + 1],
                                    ALU.subtract, ALU.mult).then_inc(xh_done, 1)
                dve.wait_ge(l_mm, CHUNKS)
                dve.wait_ge(made, 6)
                c.step(v.tensor_tensor(logits[:], ps_l[:], gate_b[:, None, :].broadcast_to([P, N, E]), ALU.add))
                c.step(v.tensor_reduce(top[:], logits[:], AX.X, ALU.max))
                c.step(v.tensor_tensor(eq[:], logits[:], top[:, :, None].broadcast_to([P, N, E]), ALU.is_equal))
                c.step(v.tensor_tensor(eq[:], eq[:], prefer[:, None, :].broadcast_to([P, N, E]), ALU.mult))
                c.step(v.tensor_reduce(top[:], eq[:], AX.X, ALU.max))
                v.tensor_tensor(hot[:], eq[:], top[:, :, None].broadcast_to([P, N, E]), ALU.is_equal).then_inc(hot_done, 1)
                dve.wait_ge(r_mm, 2)
                c.step(v.tensor_copy(count[:], ps_c[:].rearrange("p t e -> p e t")))
                c.step(v.tensor_tensor_scan(out=seen[:].rearrange("p e t -> p (e t)"),
                                            data0=restart[:].rearrange("p e t -> p (e t)"),
                                            data1=count[:].rearrange("p e t -> p (e t)"),
                                            initial=0.0, op0=ALU.mult, op1=ALU.add))
                c.step(v.tensor_scalar(tiles_i[:], seen[:, :, N - 1], float(P - 1), None, ALU.add))
                c.step(v.tensor_scalar(tiles_i[:], tiles_i[:], P.bit_length() - 1, None, ALU.logical_shift_right))
                c.step(v.tensor_copy(tiles[:], tiles_i[:]))
                c.step(v.tensor_tensor_scan(out=tile_end[:], data0=ones[:, 0:E], data1=tiles[:], initial=0.0,
                                            op0=ALU.mult, op1=ALU.add))
                c.step(v.tensor_tensor(first_slot[:], tile_end[:], tiles[:], ALU.subtract))
                c.step(v.tensor_scalar(first_slot[:], first_slot[:], float(P), None, ALU.mult))
                c.step(v.tensor_tensor(seen[:], seen[:], count[:], ALU.subtract))
                c.step(v.tensor_tensor(seen[:], seen[:], first_slot[:, :, None].broadcast_to([P, E, N]), ALU.add))
                c.step(v.tensor_tensor(eq[:], ps_r[:], seen[:].rearrange("p e t -> p t e"), ALU.add))
                c.step(v.tensor_tensor(eq[:], eq[:], hot[:], ALU.mult))
                c.step(v.tensor_reduce(top[:], eq[:], AX.X, ALU.add))
                c.step(v.tensor_copy(slot_i[:], top[:]))
                c.step(v.tensor_tensor(past[:], tile_end[:, None, 0:E - 1].broadcast_to([P, TILES, E - 1]),
                                       tile_no[:, :, None].broadcast_to([P, TILES, E - 1]), ALU.is_le))
                c.step(v.tensor_reduce(expert[:], past[:], AX.X, ALU.add))
                c.step(v.tensor_copy(expert_i[:], expert[:]))


def experts(nc, io, consts, x1, x2, xh, slot_i, expert_i, ln2_wb, w1, w2, w_ready, sorted_x, sorted_y, cleared):
    ident = consts[0]
    Q = HID // P
    LEAD = 3
    with ExitStack() as ctx:
        mem = Memory(nc, ctx)
        xt = mem.sb("xt", [P, 2, D])
        x_t = mem.sb("xT", [P, 2, P])
        hid = mem.sb("hid", [P, 2, HID])
        hid_t = mem.sb("hid_t", [P, 2, HID])
        yb = mem.sb("yb", [P, 2, D])
        ps_x = [mem.ps(f"m_x{k}", [P, 512]) for k in range(2)]
        ps_h = [mem.ps(f"m_h{k}", [P, HID]) for k in range(2)]
        ps_t = [mem.ps(f"m_t{k}", [P, HID]) for k in range(2)]
        ps_y = [mem.ps(f"m_y{k}", [P, 512]) for k in range(2)]
        names = ("sent", "loaded0", "loaded1", "x_mm", "x_out", "h_mm", "h_out", "t_mm", "t_out", "y_mm", "y_out", "stored0", "stored1",
                 "fetched", "r_mm", "r_out", "sum", "out")
        (sent, loaded0, loaded1, x_mm, x_out, h_mm, h_out, t_mm, t_out, y_mm, y_out, stored0, stored1, fetched, r_mm, r_out, summed,
         out_done) = (mem.sem("m_" + n) for n in names)
        loaded, stored = (loaded0, loaded1), (stored0, stored1)
        with nc.Block() as block:

            @block.gpsimd
            def _(pool):
                pool.wait_ge(cleared, 16)
                for t in range(N):
                    nc.gpsimd.indirect_dma_start(sorted_x, bass.IndirectOffsetOnAxis(ap=slot_i[:, t:t + 1], axis=0),
                                                 xh[:, t, :], None).then_inc(sent, 16)
                pool.wait_ge(stored0, 16 * ((TILES + 1) // 2) + 16)
                pool.wait_ge(stored1, 16 * (TILES // 2) + 16)
                pool.wait_ge(sent, 16 * N)
                for t in range(N):
                    nc.gpsimd.indirect_dma_start(xh[:, t, :], None, sorted_y,
                                                 bass.IndirectOffsetOnAxis(ap=slot_i[:, t:t + 1], axis=0)).then_inc(fetched, 16)

            @block.sync
            def _(sp):
                sp.wait_ge(sent, 16 * N)

                def load(d, k):
                    sp.wait_ge(x_mm, d + 1)
                    sp.dma_start(xt[:, k, :], sorted_x[bass.ds(d * P, P), :]).then_inc(loaded[k], 16)

                def store(d, k):
                    sp.wait_ge(y_out, d + 3)
                    sp.dma_start(sorted_y[bass.ds(d * P, P), :], yb[:, k, :]).then_inc(stored[k], 16)

                sp.sem_inc(x_mm, 2)
                for d in range(LEAD):
                    load(d, d % 2)
                with nc.sync.Fori(0, (TILES - LEAD) // 2) as i:
                    for k in range(2):
                        load(i * 2 + k + LEAD, (k + LEAD) % 2)
                        store(i * 2 + k, k)
                for d in range(TILES - LEAD, TILES):
                    store(d, d % 2)

            @block.tensor
            def _(pe):
                mm = nc.tensor.matmul
                pe.wait_ge(w_ready, 32)

                def turn(d, k, i):
                    pe.wait_ge(loaded[k], i * 16 + 16)
                    pe.wait_ge(x_out, d + 1)
                    nc.tensor.transpose(ps_x[k][:, 0:P], xt[:, k, :], ident[:]).then_inc(x_mm, 1)

                def up(d, k):
                    e = pe.value_load(expert_i[0:1, bass.ds(d, 1)], min_val=0, max_val=E_MOE - 1)
                    pe.wait_ge(x_out, d + 3)
                    pe.wait_ge(h_out, d + 1)
                    mm(ps_h[k][:], x_t[:, k, :], w1[:, bass.ds(e * HID, HID)], start=True, stop=True).then_inc(h_mm, 1)

                def turn_hidden(d, k):
                    pe.wait_ge(h_out, d + 3)
                    pe.wait_ge(t_out, d + 1)
                    for q in range(Q):
                        last = nc.tensor.transpose(ps_t[k][:, q * P:(q + 1) * P], hid[:, k, q * P:(q + 1) * P], ident[:])
                    last.then_inc(t_mm, 1)

                def down(d, k):
                    e = pe.value_load(expert_i[0:1, bass.ds(d, 1)], min_val=0, max_val=E_MOE - 1)
                    pe.wait_ge(t_out, d + 3)
                    pe.wait_ge(y_out, d + 1)
                    for q in range(Q):
                        last = mm(ps_y[k][:, 0:D], hid_t[:, k, q * P:(q + 1) * P], w2[:, bass.ds(e * (Q * D) + q * D, D)],
                                  start=q == 0, stop=q == Q - 1)
                    last.then_inc(y_mm, 1)

                def body(d, k, i, lo, hi):
                    if hi:
                        turn(d + 1, 1 - k, i + k)
                    up(d, k)
                    if lo:
                        down(d - 1, 1 - k)
                    turn_hidden(d, k)

                turn(0, 0, 0)
                body(0, 0, 0, False, True)
                body(1, 1, 0, True, True)
                with nc.tensor.Fori(1, TILES // 2) as i:
                    body(i * 2, 0, i, True, True)
                    body(i * 2 + 1, 1, i, True, True)
                body(TILES - 1, 0, TILES // 2, True, False)
                down(TILES - 1, 0)
                for c in range(CHUNKS):
                    pe.wait_ge(r_out, c + 1)
                    for k in range(TC):
                        last = nc.tensor.transpose(ps_h[c % 2][:, k * P:(k + 1) * P], x1[:, c * TC + k, :], ident[:])
                    last.then_inc(r_mm, 1)

            @block.scalar
            def _(act):
                fn = nc.scalar.activation
                act.sem_inc(x_out, 2)
                act.sem_inc(h_out, 2)

                def body(d, k):
                    act.wait_ge(x_mm, d + 3)
                    fn(x_t[:, k, :], ps_x[k][:, 0:P], ACT.Identity, scale=ln2_wb[:, 0:1],
                       bias=ln2_wb[:, 1:2]).then_inc(x_out, 1)
                    act.wait_ge(h_mm, d + 1)
                    fn(hid[:, k, :], ps_h[k][:], ACT.Gelu_apprx_tanh).then_inc(h_out, 1)

                body(0, 0)
                body(1, 1)
                with nc.scalar.Fori(1, TILES // 2) as i:
                    for k in range(2):
                        act.wait_ge(t_mm, i * 2 + k - 1)
                        body(i * 2 + k, k)
                act.wait_ge(t_mm, TILES - 2)
                body(TILES - 1, 0)

            @block.vector
            def _(dve):
                v = nc.vector
                dve.sem_inc(t_out, 2)
                dve.sem_inc(y_out, 2)
                dve.sem_inc(r_out, 2)
                for k in range(2):
                    dve.sem_inc(stored[k], 16)

                def body(d, k, i):
                    dve.wait_ge(t_mm, d + 1)
                    v.tensor_copy(hid_t[:, k, :], ps_t[k][:]).then_inc(t_out, 1)
                    dve.wait_ge(y_mm, d + 1)
                    dve.wait_ge(stored[k], i * 16 + 16)
                    v.tensor_copy(yb[:, k, :], ps_y[k][:, 0:D]).then_inc(y_out, 1)

                with nc.vector.Fori(0, TILES // 2) as i:
                    body(i * 2, 0, i)
                    body(i * 2 + 1, 1, i)
                body(TILES - 1, 0, TILES // 2)
                for c in range(CHUNKS):
                    here = x2[:, c * TC:(c + 1) * TC, :]
                    dve.wait_ge(r_mm, c + 1)
                    v.tensor_tensor(here, ps_h[c % 2][:].rearrange("p (t d) -> p t d", d=D), here, ALU.add).then_inc(r_out, 1)
                for c in range(CHUNKS):
                    here = x2[:, c * TC:(c + 1) * TC, :]
                    dve.wait_ge(r_out, c + 3)
                    if c == 0:
                        dve.wait_ge(fetched, 16 * N)
                    v.tensor_tensor(here, here, xh[:, c * TC:(c + 1) * TC, :], ALU.add).then_inc(summed, 1)

        with nc.Block() as block:

            @block.sync
            def _(sp):
                for c in range(CHUNKS):
                    sp.dma_start(io["out"].rearrange("b t d -> b (t d)")[:, c * TC * D:(c + 1) * TC * D],
                                 x2[:, c * TC:(c + 1) * TC, :].rearrange("p t d -> p (t d)")).then_inc(out_done, 16)
                sp.wait_ge(out_done, 16 * CHUNKS)


def adaln_ffn(nc, io):
    with ExitStack() as ctx:
        keep = Memory(nc, ctx)
        buf_a = keep.sb("buf_a", [P, T])
        buf_b = keep.sb("buf_b", [P, T])
        buf_x1 = keep.sb("x1", [P, N, B])
        cw_t = keep.sb("cw_t", [24, T], BF16)
        u_last = keep.sb("u_last", [P, G])
        v_last = keep.sb("v_last", [P, B])
        sorted_x = nc.dram_tensor("sorted_x", (SLOTS, D), F32, kind="Internal").ap()
        sorted_y = nc.dram_tensor("sorted_y", (SLOTS, D), F32, kind="Internal").ap()
        cleared, w_ready = keep.sem("cleared"), keep.sem("w_ready")
        consts = constants(nc, keep, keep)
        sinkhorn(nc, io, consts, buf_a, buf_b, u_last, v_last)
        plan_tokens(nc, io, consts, buf_a, buf_b, u_last, v_last, cw_t)
        routed_ffn(nc, io, buf_b, cw_t, buf_x1)
        zeros = keep.sb("zeros", [P, D])
        xn_t = keep.sb("xn_t", [P, B, N])
        o_t = keep.sb("o_t", [P, N, B])
        w1 = keep.sb("w1", [P, E_MOE * HID])
        w2 = keep.sb("w2", [P, E_MOE * HID])
        slot_i = keep.sb("slot_i", [P, N], I32)
        expert_i = keep.sb("expert_i", [P, TILES], I32)
        ln2_wb = keep.sb("ln2_wb", [P, 2])
        ys = buf_a[:].rearrange("p (t b) -> p t b", b=B)
        rows = buf_a[:].rearrange("p (t d) -> p t d", d=D)
        x2 = buf_b[:].rearrange("p (t d) -> p t d", d=D)
        clear_slots(nc, zeros, sorted_x, cleared, w1, w2, io, w_ready)
        gru(nc, io, buf_x1, ys)
        norm_first(nc, io, consts, ys, x2, xn_t)
        attention(nc, io, consts, xn_t, o_t)
        project_and_route(nc, io, consts, o_t, x2, rows, slot_i, expert_i, ln2_wb)
        experts(nc, io, consts, buf_x1, x2, rows, slot_i, expert_i, ln2_wb, w1, w2, w_ready, sorted_x, sorted_y, cleared)


def clear_slots(nc, zeros, sorted_x, cleared, w1, w2, io, w_ready):
    with ExitStack() as ctx:
        made = Memory(nc, ctx).sem("zeros_made")
        with nc.Block() as block:

            @block.gpsimd
            def _(pool):
                nc.gpsimd.memset(zeros[:], 0.0).then_inc(made, 1)

            @block.sync
            def _(sp):
                sp.dma_start(w1[:], io["w1"]).then_inc(w_ready, 16)
                sp.dma_start(w2[:], io["w2"]).then_inc(w_ready, 16)
                sp.wait_ge(made, 1)
                sp.dma_start(sorted_x.rearrange("(j p) d -> p j d", p=P),
                             zeros[:, None, :].broadcast_to([P, TILES, D])).then_inc(cleared, 16)


def kernel(**inputs):
    import numpy as np
    import concourse.bacc as bacc
    from concourse.bass_utils import run_bass_kernel_spmd as run

    a = {k: np.asarray(v) for k, v in inputs.items()}
    flat = np.ascontiguousarray
    x = a["x"].reshape(T, D)
    wz, wr, wh = (a[f"L1_cond_W{k}"] for k in "zrh")
    laid = {
        "x": x,
        "x_t": x.T,
        "cond_t": a["cond_1024"].T,
        "r_t": a["fside_BxS_0"].reshape(G, P).T,
        "gate_w0_t": a["L0_ffn_gate_weight"].T,
        "gate_b0": a["L0_ffn_gate_bias"].reshape(1, -1),
        "up0_t": np.concatenate([a["L0_ffn_up_weights"].reshape(-1, D), a["L0_ffn_shared_up_weight"]]).T,
        "down0_t": np.concatenate([a["L0_ffn_down_weights"].transpose(0, 2, 1).reshape(-1, D),
                                   a["L0_ffn_shared_down_weight"].T]),
        "gru_wx": np.concatenate([w[:D] for w in (wz, wr, wh)]),
        "gru_wh": np.concatenate([w[D:] for w in (wz, wr, wh)]),
        "gru_wp": a["L1_cond_Wp"],
        "gru_b": np.stack([a[f"L1_cond_b{k}"] for k in "zrhp"], 1),
        "ln1_wb": np.stack([a["L1_ffn_ln1_w"], a["L1_ffn_ln1_b"]], 1),
        "ln2_wb": np.stack([a["L1_ffn_ln2_w"], a["L1_ffn_ln2_b"]], 1),
        "w_qkv": a["L1_ffn_w_qkv"],
        "w_proj": a["L1_ffn_w_proj"],
        "gate_w1": a["L1_ffn_gate_w"],
        "gate_b1": a["L1_ffn_gate_b"].reshape(1, -1),
        "w1": a["L1_ffn_w1"].transpose(1, 0, 2).reshape(P, -1),
        "w2": a["L1_ffn_w2"].reshape(E_MOE, HID // P, P, D).transpose(2, 0, 1, 3).reshape(P, -1),
    }
    laid = {"in_" + k: flat(v) for k, v in laid.items()}
    nc = bacc.Bacc("TRN2", target_bir_lowering=False, num_devices=1)
    io = {k[3:]: nc.dram_tensor(k, v.shape, F32, kind="ExternalInput").ap() for k, v in laid.items()}
    io["out"] = nc.dram_tensor("out", (B, N, D), F32, kind="ExternalOutput").ap()
    adaln_ffn(nc, io)
    return run(nc, [laid], core_ids=[0]).results[0]["out"]
```

```python
import concourse.bass as bass
from concourse import mybir
from contextlib import ExitStack

F32 = mybir.dt.float32
BF16 = mybir.dt.bfloat16
I32 = mybir.dt.int32
ALU = mybir.AluOpType
ACT = mybir.ActivationFunctionType
AX = mybir.AxisListType

P = 128
B, N, D = 128, 32, 128
T = B * N
G = T // P
BG = P // N
MU, TOL, EPS, ITERS = 0.1, 1e-9, 1e-12, 31
HALF = G // 2
HB = HALF * BG


class Memory:

    def __init__(self, nc, ctx):
        self.nc, self.ctx = nc, ctx

    def sb(self, name, shape, dt=F32):
        return self.ctx.enter_context(self.nc.sbuf_tensor(name, shape, dt))

    def ps(self, name, shape, dt=F32):
        return self.ctx.enter_context(self.nc.psum_tensor(name, shape, dt))

    def sem(self, name):
        return self.ctx.enter_context(self.nc.semaphore(name))


class Chain:

    def __init__(self, eng, sem, start=0):
        self.eng, self.sem, self.n = eng, sem, start

    def step(self, ins):
        ins.then_inc(self.sem, 1)
        self.n = self.n + 1
        self.eng.wait_ge(self.sem, self.n)


def high_halves(t):
    return t[:].bitcast(BF16).rearrange("p k (m two) -> p k m two", two=2)[:, :, :, 1]


def constants(nc, mem, keep):
    ident = keep.sb("ident", [P, P])
    same_batch = keep.sb("same_batch", [P, P])
    own_batch = keep.sb("own_batch", [P, BG])
    ones = keep.sb("ones", [P, P])
    neg_tol = keep.sb("neg_tol", [P, 1])
    rounds = keep.sb("rounds", [1, ITERS])
    ident_b = keep.sb("ident_b", [P, P], BF16)
    made = mem.sem("const_made")
    with nc.Block() as block:

        @block.gpsimd
        def _(pool):
            g = nc.gpsimd
            c = Chain(pool, made)
            c.step(g.memset(ident[:], 0.0))
            c.step(g.affine_select(out=ident[:], in_=ident[:], compare_op=ALU.not_equal, fill=1.0,
                                   base=0, pattern=[[-1, P]], channel_multiplier=1))
            c.step(g.memset(ones[:], 1.0))
            c.step(g.memset(neg_tol[:], -TOL))
            c.step(g.iota(rounds[:], pattern=[[1, ITERS]], base=0, channel_multiplier=0,
                          allow_small_or_imprecise_dtypes=True))
            c.step(g.tensor_copy(ident_b[:], ident[:]))
            for t, width in ((same_batch, N), (own_batch, 1)):
                v = t[:].rearrange("p (b n) -> p b n", n=width)
                c.step(g.memset(t[:], 1.0))
                c.step(g.affine_select(out=v, in_=v, compare_op=ALU.is_ge, fill=0.0, base=0,
                                       pattern=[[-N, BG], [0, width]], channel_multiplier=1))
                c.step(g.affine_select(out=v, in_=v, compare_op=ALU.is_ge, fill=0.0, base=N - 1,
                                       pattern=[[N, BG], [0, width]], channel_multiplier=-1))
    return ident, ident_b, same_batch, own_batch, ones, neg_tol, rounds


def sinkhorn(nc, io, consts, K, KT, u_last, v_last):
    ident, ident_b, same_batch, own_batch, ones, neg_tol, rounds = consts
    with ExitStack() as ctx:
        mem = Memory(nc, ctx)
        kp = mem.sb("k_parts", [P, 3, T], BF16)
        ktp = mem.sb("kt_parts", [P, 3, T], BF16)
        rest = mem.sb("rest", [P, T])
        c_t = mem.sb("c_t", [P, B])
        r_t = mem.sb("r_t", [P, G])
        r_blk = mem.sb("r_blk", [P, G, BG])
        ksum = mem.sb("ksum", [P, G])
        ktsum = mem.sb("ktsum", [P, B])
        kinv = mem.sb("kinv", [P, G])
        ktinv = mem.sb("ktinv", [P, B])
        u3 = mem.sb("u3", [P, 3, B])
        v3 = mem.sb("v3", [P, 3, B])
        u_hist = mem.sb("u_hist", [P, ITERS + 2, B])
        v_hist = mem.sb("v_hist", [P, ITERS + 1, B])
        u_diff = mem.sb("u_diff", [P, B])
        over = mem.sb("over", [P, 2, B])
        still = mem.sb("still", [1, 2, ITERS])
        stop = mem.sb("stop", [1, 1])
        stop_i = mem.sb("stop_i", [1, 1], I32)
        moved = mem.sb("moved", [P, ITERS])
        tot = mem.sb("tot", [P, 2, HB])
        den = mem.sb("den", [P, 2, HB])
        inv = mem.sb("inv", [P, 2, HB])
        ps_v = [mem.ps(f"ps_v{h}", [P, 512]) for h in range(2)]
        ps_u = [mem.ps(f"ps_u{h}", [P, 512]) for h in range(2)]
        s = {n: mem.sem(n) for n in ("x_in", "xt_in", "cr_in", "k_exp", "kt_exp", "ksum_ready", "sums_mm",
                                     "k_scaled", "part1", "dve", "parts_ready", "v_mm", "u_mm", "v_ready", "u_ready",
                                     "v_two", "u_two", "v_kept", "u_kept", "u_read", "v_read", "diffed", "judged", "overs", "kdone")}
        xv = io["x"].rearrange("(g p) m -> p g m", p=P)
        Kv = K[:].rearrange("p (g m) -> p g m", m=D)
        KTv = KT[:].rearrange("p (b n) -> p b n", n=N)

        with nc.Block() as block:

            @block.sync
            def _(sp):
                sp.dma_start(KT[:], io["x_t"]).then_inc(s["xt_in"], 16)
                sp.dma_start(Kv, xv).then_inc(s["x_in"], 16)
                sp.dma_start(c_t[:], io["cond_t"]).then_inc(s["cr_in"], 16)
                sp.dma_start(r_t[:], io["r_t"]).then_inc(s["cr_in"], 16)

            @block.scalar
            def _(act):
                act.wait_ge(s["xt_in"], 16)
                nc.scalar.activation(KT[:], KT[:], ACT.Exp, scale=-1.0 / MU).then_inc(s["kt_exp"], 1)
                act.wait_ge(s["x_in"], 16)
                nc.scalar.activation(K[:], K[:], ACT.Exp, scale=-1.0 / MU).then_inc(s["k_exp"], 1)
                act.wait_ge(s["k_scaled"], 1)
                nc.scalar.copy(ktp[:, 0, :], KT[:]).then_inc(s["part1"], 1)
                act.wait_ge(s["k_scaled"], 2)
                nc.scalar.copy(kp[:, 0, :], K[:]).then_inc(s["part1"], 1)

            @block.tensor
            def _(pe):
                pe.wait_ge(s["ksum_ready"], 1)
                nc.tensor.matmul(ps_v[0][:, 0:B], ones[:], ktsum[:], start=True, stop=True).then_inc(s["sums_mm"], 1)
                pe.wait_ge(s["ksum_ready"], 2)
                nc.tensor.matmul(ps_v[1][:, 0:G], same_batch[:], ksum[:], start=True, stop=True).then_inc(s["sums_mm"], 1)

            @block.vector
            def _(dve):
                v = nc.vector
                c = Chain(dve, s["dve"])
                dve.wait_ge(s["kt_exp"], 1)
                v.tensor_reduce(ktsum[:], KTv, AX.X, ALU.add).then_inc(s["ksum_ready"], 1)
                dve.wait_ge(s["k_exp"], 1)
                v.tensor_reduce(ksum[:], Kv, AX.X, ALU.add).then_inc(s["ksum_ready"], 1)
                dve.wait_ge(s["sums_mm"], 1)
                c.step(v.tensor_scalar(ktinv[:], ps_v[0][:, 0:B], EPS, None, ALU.max))
                c.step(v.reciprocal(ktinv[:], ktinv[:]))
                dve.wait_ge(s["cr_in"], 32)
                c.step(v.tensor_tensor(ktinv[:], ktinv[:], c_t[:], ALU.mult))
                v.tensor_tensor(KTv, KTv, ktinv[:, :, None].broadcast_to([P, B, N]), ALU.mult).then_inc(s["k_scaled"], 1)
                dve.wait_ge(s["sums_mm"], 2)
                c.step(v.tensor_scalar(kinv[:], ps_v[1][:, 0:G], EPS, None, ALU.max))
                c.step(v.reciprocal(kinv[:], kinv[:]))
                v.tensor_tensor(Kv, Kv, kinv[:, :, None].broadcast_to([P, G, D]), ALU.mult).then_inc(s["k_scaled"], 1)
                for n, (whole, parts) in enumerate(((KT, ktp), (K, kp))):
                    dve.wait_ge(s["k_scaled"], n + 1)
                    dve.wait_ge(s["part1"], n + 1)
                    c.step(v.tensor_tensor(rest[:], whole[:], parts[:, 0, :], ALU.subtract))
                    c.step(v.tensor_copy(parts[:, 1, :], rest[:]))
                    c.step(v.tensor_tensor(parts[:, 2, :], rest[:], parts[:, 1, :], ALU.subtract))
                dve.wait_ge(s["cr_in"], 32)
                c.step(v.tensor_tensor(r_blk[:], r_t[:, :, None].broadcast_to([P, G, BG]),
                                       own_batch[:, None, :].broadcast_to([P, G, BG]), ALU.mult))
                c.step(v.tensor_copy(u3[:, 0, :], r_blk[:].rearrange("p g b -> p (g b)")))
                c.step(v.tensor_tensor(u3[:, 1, :], u3[:, 0, :], high_halves(u3)[:, 0, :], ALU.subtract))
                c.step(v.tensor_tensor(u3[:, 2, :], u3[:, 1, :], high_halves(u3)[:, 1, :], ALU.subtract))
                c.step(v.tensor_copy(u_hist[:, 0, :].rearrange("p (g b) -> p g b", b=BG),
                                     own_batch[:, None, :].broadcast_to([P, G, BG])))
                c.step(v.tensor_copy(u_hist[:, 1, :], u3[:, 0, :]))
                c.step(v.memset(v_hist[:, 0, :], 0.0))

        ends = {}
        with nc.Block() as block:

            @block.tensor
            def _(pe):
                uh, vh = high_halves(u3), high_halves(v3)

                def products(out, parts, moving, h, done):
                    for g in range(HALF):
                        gg = h * HALF + g
                        for part in range(3):
                            last = nc.tensor.matmul(out[:, 12 * g:12 * g + 12], parts[:, part, gg * P:(gg + 1) * P],
                                                    moving[:, :, gg * BG:(gg + 1) * BG],
                                                    start=part == 0, stop=part == 2)
                    last.then_inc(done, 1)

                with nc.tensor.Fori(0, ITERS) as i:
                    for h in range(2):
                        pe.wait_ge(s["u_ready"], i * 2 + h + 1)
                        products(ps_v[h], kp, uh, h, s["v_mm"])
                    for h in range(2):
                        pe.wait_ge(s["v_ready"], i * 2 + h + 1)
                        products(ps_u[h], ktp, vh, h, s["u_mm"])

            @block.vector
            def _(dve):
                v = nc.vector
                uh, vh = high_halves(u3), high_halves(v3)
                dve.sem_inc(s["u_ready"], 2)

                def scaled(ps, h, num, out3, highs, chain, done):
                    cols = slice(h * HB, (h + 1) * HB)
                    chain.step(v.tensor_reduce(tot[:, h, :], ps[:, 0:12 * HALF].rearrange("p (g k b) -> p g b k", k=3, b=BG),
                                               AX.X, ALU.add))
                    chain.step(v.tensor_scalar(den[:, h, :], tot[:, h, :], EPS, None, ALU.max))
                    if num is None:
                        chain.step(v.reciprocal(out3[:, 0, cols], den[:, h, :]))
                    else:
                        chain.step(v.reciprocal(inv[:, h, :], den[:, h, :]))
                        chain.step(v.tensor_tensor(out3[:, 0, cols], inv[:, h, :], num[:, cols], ALU.mult))
                    v.tensor_tensor(out3[:, 1, cols], out3[:, 0, cols], highs[:, 0, cols], ALU.subtract).then_inc(done, 1)

                base = 18
                r_flat = r_blk[:].rearrange("p g b -> p (g b)")
                with nc.vector.Fori(0, ITERS) as i:
                    c = Chain(dve, s["dve"], i * 14 + base)
                    for h in range(2):
                        dve.wait_ge(s["v_mm"], i * 2 + h + 1)
                        dve.wait_ge(s["v_kept"], i * 2 + h + 1)
                        scaled(ps_v[h], h, None, v3, vh, c, s["v_two"])
                    for h in range(2):
                        dve.wait_ge(s["u_mm"], i * 2 + h + 1)
                        dve.wait_ge(s["u_kept"], i * 2 + h + 1)
                        scaled(ps_u[h], h, r_flat, u3, uh, c, s["u_two"])

            @block.gpsimd
            def _(pool):
                g = nc.gpsimd
                vh, uh = high_halves(v3), high_halves(u3)
                pool.sem_inc(s["u_read"], 1)
                with nc.gpsimd.Fori(0, ITERS) as i:
                    for two, t3, high, ready in (("v_two", v3, vh, "v_ready"), ("u_two", u3, uh, "u_ready")):
                        for h in range(2):
                            cols = slice(h * HB, (h + 1) * HB)
                            pool.wait_ge(s[two], i * 2 + h + 1)
                            g.tensor_tensor(t3[:, 2, cols], t3[:, 1, cols], high[:, 1, cols],
                                            ALU.subtract).then_inc(s[ready], 1)
                        if t3 is v3:
                            pool.wait_ge(s["u_kept"], i * 2 + 2)
                            pool.wait_ge(s["u_read"], i + 1)
                            g.tensor_tensor(u_diff[:], u_hist[:, i + 1, :], u_hist[:, i, :],
                                            ALU.subtract).then_inc(s["diffed"], 1)

            @block.scalar
            def _(act):
                act.sem_inc(s["v_kept"], 2)
                act.sem_inc(s["u_kept"], 2)
                with nc.scalar.Fori(0, ITERS) as i:
                    for h in range(2):
                        cols = slice(h * HB, (h + 1) * HB)
                        act.wait_ge(s["v_two"], i * 2 + h + 1)
                        nc.scalar.copy(v_hist[:, i + 1, cols], v3[:, 0, cols]).then_inc(s["v_kept"], 1)
                    act.wait_ge(s["diffed"], i + 1)
                    nc.scalar.activation(over[:, 0, :], u_diff[:], ACT.Abs).then_inc(s["u_read"], 1)
                    act.wait_ge(s["u_read"], i + 2)
                    nc.scalar.activation(over[:, 1, :], over[:, 0, :], ACT.Relu, bias=neg_tol[:],
                                         accum_out=moved[:, bass.ds(i, 1)]).then_inc(s["judged"], 1)
                    act.wait_ge(s["judged"], i + 1)
                    for h in range(2):
                        cols = slice(h * HB, (h + 1) * HB)
                        act.wait_ge(s["u_two"], i * 2 + h + 1)
                        nc.scalar.copy(u_hist[:, i + 2, cols], u3[:, 0, cols]).then_inc(s["u_kept"], 1)

        with nc.Block() as block:

            @block.tensor
            def _(pe):
                nc.tensor.matmul(ps_v[0][0:1, 0:ITERS], ones[:, 0:1], moved[:], start=True, stop=True).then_inc(s["overs"], 1)

            @block.vector
            def _(dve):
                v = nc.vector
                c = Chain(dve, s["kdone"])
                dve.wait_ge(s["overs"], 1)
                c.step(v.tensor_scalar(still[:, 0, :], ps_v[0][0:1, 0:ITERS], 0.0, float(2 * ITERS), ALU.is_gt, ALU.mult))
                c.step(v.tensor_tensor(still[:, 1, :], still[:, 0, :], rounds[:], ALU.add))
                c.step(v.tensor_reduce(stop[:], still[:, 1, :], AX.X, ALU.min))
                c.step(v.tensor_scalar(stop_i[:], stop[:], float(ITERS), None, ALU.min))
                k = v.value_load(stop_i[0:1, 0:1], min_val=0, max_val=ITERS)
                c.step(v.tensor_reduce(u_last[:], u_hist[:, k + 1, :].rearrange("p (g b) -> p g b", b=BG), AX.X, ALU.add))
                c.step(v.tensor_tensor(v_last[:], v_hist[:, k, :], c_t[:], ALU.mult))


def plan_tokens(nc, io, consts, K, KT, u_last, v_last, cw_t):
    ident, ident_b = consts[0], consts[1]
    E, GE = 8, 4
    CH = 4
    with ExitStack() as ctx:
        mem = Memory(nc, ctx)
        gate_w = mem.sb("gate_w", [P, E])
        gate_b = mem.sb("gate_b", [P, E])
        prefer = mem.sb("prefer", [P, E])
        scores = mem.sb("scores", [P, G, E])
        biased = mem.sb("biased", [P, G, E])
        pair_hi = mem.sb("pair_hi", [P, 2 * G, 2])
        pair_lo = mem.sb("pair_lo", [P, 2 * G, 2])
        best = mem.sb("best", [P, 2 * G])
        second = mem.sb("second", [P, 2 * G])
        third = mem.sb("third", [P, 2 * G])
        gmask = mem.sb("gmask", [P, G, 2])
        eq = mem.sb("eq", [P, G, E])
        top = mem.sb("top", [P, G])
        hot = mem.sb("hot", [P, 2, G, E])
        cw = mem.sb("cw", [P, G, E])
        cw_left = mem.sb("cw_left", [P, G, E])
        cw_parts = mem.sb("cw_parts", [P, G, E, 3], BF16)
        ps_t = [mem.ps(f"ps_t{h}", [P, 512]) for h in range(2)]
        ps_l = mem.ps("ps_l", [P, G, E])
        ps_c = [mem.ps(f"ps_c{h}", [3 * E, 1024], BF16) for h in range(2)]
        gate_in, pref, scaled, t_mm, pt_ready, l_mm, scored, dve_s, split, c_mm, c_copied = (
            mem.sem(n) for n in ("gate_in", "pref", "scaled", "t_mm", "pt_ready", "l_mm", "scored", "rt_dve", "split",
                                 "c_mm", "c_copied"))
        with nc.Block() as block:

            @block.sync
            def _(sp):
                sp.dma_start(gate_w[:], io["gate_w0_t"]).then_inc(gate_in, 16)
                sp.dma_start(gate_b[:], io["gate_b0"].broadcast_to([P, E])).then_inc(gate_in, 16)

            @block.gpsimd
            def _(pool):
                nc.gpsimd.iota(prefer[:], pattern=[[-1, E]], base=E, channel_multiplier=0,
                               allow_small_or_imprecise_dtypes=True).then_inc(pref, 1)

            @block.tensor
            def _(pe):
                pe.wait_ge(gate_in, 32)
                for c in range(G // CH):
                    pe.wait_ge(scaled, c + 1)
                    if c >= 2:
                        pe.wait_ge(pt_ready, c - 1)
                    for g in range(CH):
                        gg = c * CH + g
                        last = nc.tensor.transpose(ps_t[c % 2][:, g * P:(g + 1) * P], K[:, gg * P:(gg + 1) * P], ident[:])
                    last.then_inc(t_mm, 1)
                for c in range(G // CH):
                    pe.wait_ge(pt_ready, c + 1)
                    for gg in range(c * CH, (c + 1) * CH):
                        last = nc.tensor.matmul(ps_l[:, gg, :], KT[:, gg * P:(gg + 1) * P], gate_w[:], start=True, stop=True)
                last.then_inc(l_mm, 1)
                pe.wait_ge(split, 1)
                for c in range(G // 8):
                    if c >= 2:
                        pe.wait_ge(c_copied, c - 1)
                    for g in range(8):
                        last = nc.tensor.transpose(ps_c[c % 2][:, g * P:(g + 1) * P],
                                                   cw_parts[:, c * 8 + g].rearrange("p e k -> p (e k)"), ident_b[:])
                    last.then_inc(c_mm, 1)

            @block.scalar
            def _(act):
                act.wait_ge(l_mm, 1)
                nc.scalar.activation(scores[:], ps_l[:], ACT.Sigmoid).then_inc(scored, 1)
                for c in range(G // 8):
                    act.wait_ge(c_mm, c + 1)
                    nc.scalar.copy(cw_t[:, c * 1024:(c + 1) * 1024], ps_c[c % 2][:]).then_inc(c_copied, 1)

            @block.vector
            def _(dve):
                v = nc.vector
                Kv = K[:].rearrange("p (g m) -> p g m", m=D)
                W = CH * P
                NB = CH * BG
                for c in range(G // CH + 1):
                    if c < G // CH:
                        v.tensor_tensor(Kv[:, c * CH:(c + 1) * CH, :], Kv[:, c * CH:(c + 1) * CH, :],
                                        u_last[:, c * CH:(c + 1) * CH, None].broadcast_to([P, CH, D]),
                                        ALU.mult).then_inc(scaled, 1)
                    if c >= 1:
                        b = c - 1
                        dve.wait_ge(t_mm, b + 1)
                        v.tensor_tensor(KT[:, b * W:(b + 1) * W].rearrange("p (b n) -> p b n", n=N),
                                        ps_t[b % 2][:].rearrange("p (b n) -> p b n", n=N),
                                        v_last[:, b * NB:(b + 1) * NB, None].broadcast_to([P, NB, N]),
                                        ALU.mult).then_inc(pt_ready, 1)
                c = Chain(dve, dve_s)
                dve.wait_ge(scored, 1)
                dve.wait_ge(pref, 1)
                dve.wait_ge(gate_in, 32)
                c.step(v.tensor_tensor(biased[:], scores[:], gate_b[:, None, :].broadcast_to([P, G, E]), ALU.add))
                quad = biased[:].rearrange("p g (q h w) -> p (g q) h w", q=2, w=2)
                c.step(v.tensor_tensor(pair_hi[:], quad[:, :, :, 0], quad[:, :, :, 1], ALU.max))
                c.step(v.tensor_tensor(pair_lo[:], quad[:, :, :, 0], quad[:, :, :, 1], ALU.min))
                c.step(v.tensor_tensor(best[:], pair_hi[:, :, 0], pair_hi[:, :, 1], ALU.max))
                c.step(v.tensor_tensor(second[:], pair_hi[:, :, 0], pair_hi[:, :, 1], ALU.min))
                c.step(v.tensor_tensor(third[:], pair_lo[:, :, 0], pair_lo[:, :, 1], ALU.max))
                c.step(v.tensor_tensor(second[:], second[:], third[:], ALU.max))
                c.step(v.tensor_tensor(best[:], best[:], second[:], ALU.add))
                gs = best[:].rearrange("p (g q) -> p g q", q=2)
                c.step(v.tensor_tensor(gmask[:, :, 0], gs[:, :, 0], gs[:, :, 1], ALU.is_ge))
                c.step(v.tensor_tensor(gmask[:, :, 1], gs[:, :, 0], gs[:, :, 1], ALU.is_lt))
                c.step(v.tensor_tensor(biased[:].rearrange("p g (q w) -> p (g q) w", q=2),
                                       biased[:].rearrange("p g (q w) -> p (g q) w", q=2),
                                       gmask[:].rearrange("p g q -> p (g q)")[:, :, None].broadcast_to([P, 2 * G, GE]), ALU.mult))
                for n in range(2):
                    c.step(v.tensor_reduce(top[:], biased[:], AX.X, ALU.max))
                    c.step(v.tensor_tensor(eq[:], biased[:], top[:, :, None].broadcast_to([P, G, E]), ALU.is_equal))
                    c.step(v.tensor_tensor(eq[:], eq[:], prefer[:, None, :].broadcast_to([P, G, E]), ALU.mult))
                    c.step(v.tensor_reduce(top[:], eq[:], AX.X, ALU.max))
                    c.step(v.tensor_tensor(hot[:, n], eq[:], top[:, :, None].broadcast_to([P, G, E]), ALU.is_equal))
                    if n == 0:
                        c.step(v.scalar_tensor_tensor(out=biased[:], in0=hot[:, 0], scalar=-1e30, in1=biased[:],
                                                      op0=ALU.mult, op1=ALU.add))
                c.step(v.tensor_tensor(hot[:, 0], hot[:, 0], hot[:, 1], ALU.add))
                c.step(v.tensor_tensor(cw[:], hot[:, 0], scores[:], ALU.mult))
                c.step(v.tensor_reduce(top[:], cw[:], AX.X, ALU.add))
                c.step(v.tensor_scalar(top[:], top[:], 1e-20, None, ALU.add))
                c.step(v.reciprocal(top[:], top[:]))
                c.step(v.tensor_tensor(cw[:], cw[:], top[:, :, None].broadcast_to([P, G, E]), ALU.mult))
                c.step(v.tensor_scalar(cw[:], cw[:], 2.5, None, ALU.mult))
                c.step(v.tensor_copy(cw_parts[:, :, :, 0], cw[:]))
                c.step(v.tensor_tensor(cw_left[:], cw[:], cw_parts[:, :, :, 0], ALU.subtract))
                c.step(v.tensor_copy(cw_parts[:, :, :, 1], cw_left[:]))
                v.tensor_tensor(cw_parts[:, :, :, 2], cw_left[:], cw_parts[:, :, :, 1], ALU.subtract).then_inc(split, 1)


def routed_ffn(nc, io, PT, cw_t, x1):
    J, JR = 6, 4
    W, NB = 512, 512 // N
    with ExitStack() as ctx:
        mem = Memory(nc, ctx)
        up = mem.sb("up0", [P, J * P])
        down = mem.sb("down0", [P, J, D])
        spread = mem.sb("spread", [24, JR, 2, 64], BF16)
        x_t2 = mem.sb("x_t2", [P, T])
        relu = mem.sb("relu", [P, 2, W])
        rc = mem.sb("rc", [P, W])
        gated = mem.sb("gated", [P, 2, W])
        ps_h = [mem.ps(f"ps_h{h}", [P, W]) for h in range(2)]
        ps_c = [mem.ps(f"ps_cw{h}", [P, W]) for h in range(2)]
        ps_y = [mem.ps(f"ps_y{h}", [P, W]) for h in range(2)]
        w_in, made, h_mm, c_mm, h_read, relu_ready, c_read, relu_read, g_ready, g_read, y_read = (
            mem.sem(n) for n in ("f_w_in", "f_made", "f_h_mm", "f_c_mm", "f_h_read", "f_relu_ready", "f_c_read",
                                 "f_relu_read", "f_g_ready", "f_g_read", "f_y_read"))
        with nc.Block() as block:

            @block.sync
            def _(sp):
                sp.dma_start(up[:], io["up0_t"]).then_inc(w_in, 16)
                sp.dma_start(down[:], io["down0_t"].rearrange("(j p) d -> p j d", p=P)).then_inc(w_in, 16)
                sp.dma_start(x_t2[:], io["x_t"]).then_inc(w_in, 16)

            @block.gpsimd
            def _(pool):
                g = nc.gpsimd
                c = Chain(pool, made)
                c.step(g.memset(spread[:], 1.0))
                c.step(g.affine_select(out=spread[:], in_=spread[:], compare_op=ALU.is_ge, fill=0.0, base=0,
                                       pattern=[[-6, JR], [-3, 2], [0, 64]], channel_multiplier=1))
                c.step(g.affine_select(out=spread[:], in_=spread[:], compare_op=ALU.is_ge, fill=0.0, base=2,
                                       pattern=[[6, JR], [3, 2], [0, 64]], channel_multiplier=-1))

            @block.tensor
            def _(pe):
                pe.wait_ge(w_in, 48)
                pe.wait_ge(made, 3)
                with nc.tensor.Fori(0, T // W // 2) as q:
                    for half in range(2):
                        tok = bass.ds(q * (2 * W) + half * W, W)
                        c = q * 2 + half
                        for j in range(J + 1):
                            if j < JR:
                                pe.wait_ge(c_read, c * JR + j + 1)
                            if j < J:
                                pe.wait_ge(h_read, c * J + j + 1)
                                nc.tensor.matmul(ps_h[j % 2][:], up[:, j * P:(j + 1) * P], PT[:, tok],
                                                 start=True, stop=True).then_inc(h_mm, 1)
                            if j < JR:
                                nc.tensor.matmul(ps_c[j % 2][:], spread[:, j].rearrange("p a b -> p (a b)"), cw_t[:, tok],
                                                 start=True, stop=True).then_inc(c_mm, 1)
                            if j >= 1:
                                i = j - 1
                                if i == 0:
                                    pe.wait_ge(y_read, c + 1)
                                pe.wait_ge(g_ready, c * J + i + 1)
                                nc.tensor.matmul(ps_y[half][:], down[:, i, :], gated[:, i % 2, :],
                                                 start=i == 0, stop=i == J - 1).then_inc(g_read, 1)

            @block.scalar
            def _(act):
                act.sem_inc(h_read, 2)
                with nc.scalar.Fori(0, T // W) as c:
                    for j in range(J):
                        act.wait_ge(h_mm, c * J + j + 1)
                        act.wait_ge(relu_read, c * J + j + 1)
                        nc.scalar.activation(relu[:, j % 2, :], ps_h[j % 2][:], ACT.Relu).then_inc(h_read, 1)

            @block.vector
            def _(dve):
                v = nc.vector
                dve.sem_inc(relu_read, 2)
                dve.sem_inc(c_read, 2)
                dve.sem_inc(g_read, 2)
                dve.sem_inc(y_read, 2)
                dve.wait_ge(w_in, 48)
                with nc.vector.Fori(0, T // W // 2) as q:
                    for half in range(2):
                        c = q * 2 + half
                        for j in range(J):
                            dve.wait_ge(h_read, c * J + j + 3)
                            other = relu[:, j % 2, :]
                            if j < JR:
                                dve.wait_ge(c_mm, c * JR + j + 1)
                                v.tensor_tensor(rc[:], relu[:, j % 2, :], ps_c[j % 2][:], ALU.mult).then_inc(c_read, 1)
                                dve.wait_ge(c_read, c * JR + j + 3)
                                other = rc[:]
                            dve.wait_ge(g_read, c * J + j + 1)
                            v.tensor_tensor(gated[:, j % 2, :], relu[:, j % 2, :], other, ALU.mult).then_inc(g_ready, 1)
                            dve.wait_ge(g_ready, c * J + j + 1)
                            dve.sem_inc(relu_read, 1)
                        dve.wait_ge(g_read, c * J + J + 2)
                        v.tensor_tensor(x1[:, :, bass.ds(q * (2 * NB) + half * NB, NB)].rearrange("p n b -> p b n"),
                                        ps_y[half][:].rearrange("p (b n) -> p b n", n=N),
                                        x_t2[:, bass.ds(q * (2 * W) + half * W, W)].rearrange("p (b n) -> p b n", n=N),
                                        ALU.add).then_inc(y_read, 1)


def gru(nc, io, x1, ys):
    STEPS = 4
    Z, R, C = range(3)
    with ExitStack() as ctx:
        mem = Memory(nc, ctx)
        wx = mem.sb("gru_wx", [P, 3, D])
        wh = mem.sb("gru_wh", [P, 3, D])
        wp = mem.sb("gru_wp", [P, D])
        bias = mem.sb("gru_b", [P, 4])
        h_in = mem.sb("h_in", [P, B])
        gate = mem.sb("gate", [P, 3, B])
        rh = mem.sb("rh", [P, B])
        zh = mem.sb("zh", [P, B])
        kept = mem.sb("kept", [P, B])
        fresh = mem.sb("fresh", [P, B])
        ps = [[mem.ps(f"ps_g{n}{k}", [P, B * 4]) for k in range(2)] for n in range(3)]
        ps_p = mem.ps("ps_prop", [P, 512])
        w_in, gates_mm, c_mm, p_mm, r_done, z_done, c_done, h_done, rh_done, y_done, own = (
            mem.sem(n) for n in ("g_w_in", "g_gates_mm", "g_c_mm", "g_p_mm", "g_r_done", "g_z_done", "g_c_done",
                                 "g_h_done", "g_rh_done", "g_y_done", "g_own"))
        with nc.Block() as block:

            @block.sync
            def _(sp):
                sp.dma_start(wx[:], io["gru_wx"].rearrange("(g p) d -> p g d", p=P)).then_inc(w_in, 16)
                sp.dma_start(wh[:], io["gru_wh"].rearrange("(g p) d -> p g d", p=P)).then_inc(w_in, 16)
                sp.dma_start(wp[:], io["gru_wp"]).then_inc(w_in, 16)
                sp.dma_start(bias[:], io["gru_b"]).then_inc(w_in, 16)
                sp.dma_start(h_in[:], io["cond_t"]).then_inc(w_in, 16)

            @block.tensor
            def _(pe):
                mm = nc.tensor.matmul

                def from_x(t, k):
                    for n in (R, Z, C):
                        mm(ps[n][k][:, 0:B], wx[:, n, :], x1[:, t, :], start=True, stop=False)

                def chunk(q, last_chunk):
                    for k in range(STEPS):
                        t = q * STEPS + k
                        if k == 0:
                            if last_chunk or not isinstance(q, int):
                                pe.wait_ge(h_done, q)
                            h = h_in[:]
                        else:
                            pe.wait_ge(y_done, t)
                            h = ys[:, t - 1, :]
                        mm(ps[R][k % 2][:, 0:B], wh[:, R, :], h, start=False, stop=True).then_inc(gates_mm, 1)
                        mm(ps[Z][k % 2][:, 0:B], wh[:, Z, :], h, start=False, stop=True).then_inc(gates_mm, 1)
                        if not (last_chunk and k == STEPS - 1):
                            from_x(t + 1, (k + 1) % 2)
                        pe.wait_ge(rh_done, t + 1)
                        mm(ps[C][k % 2][:, 0:B], wh[:, C, :], rh[:], start=False, stop=True).then_inc(c_mm, 1)
                    if not last_chunk:
                        pe.wait_ge(y_done, q * STEPS + STEPS)
                        mm(ps_p[:, 0:B], wp[:], ys[:, q * STEPS + STEPS - 1, :], start=True, stop=True).then_inc(p_mm, 1)

                pe.wait_ge(w_in, 80)
                from_x(0, 0)
                chunk(0, False)
                with nc.tensor.Fori(1, N // STEPS - 1) as q:
                    chunk(q, False)
                chunk(N // STEPS - 1, True)

            @block.scalar
            def _(act):
                fn = nc.scalar.activation

                def chunk(q, last_chunk):
                    for k in range(STEPS):
                        t = q * STEPS + k
                        act.wait_ge(gates_mm, t * 2 + 1)
                        fn(gate[:, R, :], ps[R][k % 2][:, 0:B], ACT.Sigmoid, bias=bias[:, R:R + 1]).then_inc(r_done, 1)
                        act.wait_ge(gates_mm, t * 2 + 2)
                        fn(gate[:, Z, :], ps[Z][k % 2][:, 0:B], ACT.Sigmoid, bias=bias[:, Z:Z + 1]).then_inc(z_done, 1)
                        act.wait_ge(c_mm, t + 1)
                        fn(gate[:, C, :], ps[C][k % 2][:, 0:B], ACT.Tanh, bias=bias[:, C:C + 1]).then_inc(c_done, 1)
                    if not last_chunk:
                        act.wait_ge(p_mm, q + 1)
                        fn(h_in[:], ps_p[:, 0:B], ACT.Tanh, bias=bias[:, 3:4]).then_inc(h_done, 1)

                act.wait_ge(w_in, 80)
                chunk(0, False)
                with nc.scalar.Fori(1, N // STEPS - 1) as q:
                    chunk(q, False)
                chunk(N // STEPS - 1, True)

            @block.vector
            def _(dve):
                tt = nc.vector.tensor_tensor

                def chunk(q, first):
                    for k in range(STEPS):
                        t = q * STEPS + k
                        c = Chain(dve, own, t * 3)
                        dve.wait_ge(r_done, t + 1)
                        if k == 0:
                            if not first:
                                dve.wait_ge(h_done, q)
                            h = h_in[:]
                        else:
                            dve.wait_ge(y_done, t)
                            h = ys[:, t - 1, :]
                        tt(rh[:], gate[:, R, :], h, ALU.mult).then_inc(rh_done, 1)
                        dve.wait_ge(z_done, t + 1)
                        c.step(tt(zh[:], gate[:, Z, :], h, ALU.mult))
                        c.step(tt(kept[:], h, zh[:], ALU.subtract))
                        dve.wait_ge(c_done, t + 1)
                        c.step(tt(fresh[:], gate[:, Z, :], gate[:, C, :], ALU.mult))
                        tt(ys[:, t, :], kept[:], fresh[:], ALU.add).then_inc(y_done, 1)

                dve.wait_ge(w_in, 80)
                chunk(0, True)
                with nc.vector.Fori(1, N // STEPS) as q:
                    chunk(q, False)


class NormStats:

    def __init__(self, mem, name):
        self.six = mem.sb(name + "_six", [P, N, 6])
        self.mean = mem.sb(name + "_mean", [P, N])
        self.var = mem.sb(name + "_var", [P, N])
        self.a = mem.sb(name + "_a", [P, N])
        self.root = mem.sb(name + "_root", [P, N])
        self.rstd = mem.sb(name + "_rstd", [P, N])

    def variance(self, v, c):
        s = self.six
        c.step(v.tensor_tensor(self.mean[:], s[:, :, 1], s[:, :, 4], ALU.add))
        c.step(v.tensor_tensor(self.a[:], s[:, :, 1], s[:, :, 4], ALU.subtract))
        c.step(v.tensor_tensor(self.a[:], self.a[:], self.a[:], ALU.mult))
        c.step(v.tensor_scalar(self.a[:], self.a[:], 0.25, LN_EPS, ALU.mult, ALU.add))
        c.step(v.tensor_tensor(self.var[:], s[:, :, 2], s[:, :, 5], ALU.add))
        c.step(v.tensor_scalar(self.mean[:], self.mean[:], 0.5, None, ALU.mult))
        c.step(v.scalar_tensor_tensor(out=self.var[:], in0=self.var[:], scalar=1.0 / D, in1=self.a[:],
                                      op0=ALU.mult, op1=ALU.add))

    def inverse_root(self, v, c):
        c.step(v.reciprocal(self.rstd[:], self.root[:]))
        c.step(v.tensor_tensor(self.a[:], self.rstd[:], self.rstd[:], ALU.mult))
        c.step(v.tensor_tensor(self.a[:], self.a[:], self.var[:], ALU.mult))
        c.step(v.tensor_scalar(self.a[:], self.a[:], -0.5, 1.5, ALU.mult, ALU.add))
        c.step(v.tensor_tensor(self.rstd[:], self.rstd[:], self.a[:], ALU.mult))


LN_EPS = 1e-5
TC = 4
CHUNKS = N // TC


def norm_first(nc, io, consts, ys, y_nat, xn_t):
    ident = consts[0]
    with ExitStack() as ctx:
        mem = Memory(nc, ctx)
        st = NormStats(mem, "ln1")
        wb = mem.sb("ln1_wb", [P, 2])
        xh = mem.sb("ln1_xh", [P, N, D])
        ps_n = [mem.ps(f"ps_n{k}", [P, TC * D]) for k in range(2)]
        ps_x = [mem.ps(f"ps_x{k}", [P, TC * B]) for k in range(2)]
        wb_in, y_mm, y_out, stats, own, rooted, xh_done, x_mm, x_out = (
            mem.sem("a_" + n) for n in ("wb_in", "y_mm", "y_out", "stats", "own", "rooted", "xh_done", "x_mm", "x_out"))
        with nc.Block() as block:

            @block.sync
            def _(sp):
                sp.dma_start(wb[:], io["ln1_wb"]).then_inc(wb_in, 16)

            @block.tensor
            def _(pe):
                for c in range(CHUNKS):
                    if c >= 2:
                        pe.wait_ge(y_out, c - 1)
                    for k in range(TC):
                        last = nc.tensor.transpose(ps_n[c % 2][:, k * D:(k + 1) * D], ys[:, c * TC + k, :], ident[:])
                    last.then_inc(y_mm, 1)
                for c in range(CHUNKS):
                    pe.wait_ge(xh_done, (c + 1) * TC)
                    if c >= 2:
                        pe.wait_ge(x_out, c - 1)
                    for k in range(TC):
                        last = nc.tensor.transpose(ps_x[c % 2][:, k * B:(k + 1) * B], xh[:, c * TC + k, :], ident[:])
                    last.then_inc(x_mm, 1)

            @block.scalar
            def _(act):
                with nc.scalar.Fori(0, CHUNKS // 2) as q:
                    for k in range(2):
                        act.wait_ge(y_mm, q * 2 + k + 1)
                        nc.scalar.copy(y_nat[:, bass.ds((q * 2 + k) * TC, TC), :],
                                       ps_n[k][:].rearrange("p (t d) -> p t d", d=D)).then_inc(y_out, 1)
                act.wait_ge(stats, 1)
                nc.scalar.activation(st.root[:], st.var[:], ACT.Sqrt).then_inc(rooted, 1)
                act.wait_ge(wb_in, 16)
                with nc.scalar.Fori(0, CHUNKS // 2) as q:
                    for k in range(2):
                        act.wait_ge(x_mm, q * 2 + k + 1)
                        nc.scalar.activation(xn_t[:, :, bass.ds((q * 2 + k) * TC, TC)].rearrange("p b t -> p t b"),
                                             ps_x[k][:].rearrange("p (t b) -> p t b", b=B),
                                             ACT.Identity, scale=wb[:, 0:1], bias=wb[:, 1:2]).then_inc(x_out, 1)

            @block.vector
            def _(dve):
                v = nc.vector
                with nc.vector.Fori(0, CHUNKS) as q:
                    dve.wait_ge(y_out, q + 1)
                    for k in range(TC):
                        last = v.bn_stats(st.six[:, q * TC + k, :], y_nat[:, q * TC + k, :])
                    last.then_inc(own, 1)
                c = Chain(dve, own, CHUNKS)
                dve.wait_ge(own, CHUNKS)
                st.variance(v, c)
                dve.sem_inc(stats, 1)
                dve.wait_ge(rooted, 1)
                st.inverse_root(v, c)
                for t in range(N):
                    v.tensor_scalar(xh[:, t, :], y_nat[:, t, :], st.mean[:, t:t + 1], st.rstd[:, t:t + 1],
                                    ALU.subtract, ALU.mult).then_inc(xh_done, 1)


def attention(nc, io, consts, xn_t, o_t):
    ident = consts[0]
    CB = 8
    NC = B // CB
    GR = CB // BG
    J, R, DK = 4, 4, 8
    CT = CB * N
    SCALE = 1.0 / float(DK) ** 0.5
    with ExitStack() as ctx:
        mem = Memory(nc, ctx)
        w_qkv = mem.sb("w_qkv", [P, 3, D])
        block_mask = mem.sb("block_mask", [P, J, R])
        head_mask = mem.sb("head_mask", [P, J])
        warm = mem.sb("warm", [P, 1])
        qs = mem.sb("qs", [P, CB, N])
        km = mem.sb("km", [P, CB, J, N])
        vb = mem.sb("vb", [P, 2, CB, J, R, DK])
        most = mem.sb("most", [P, R, GR * J])
        total = mem.sb("total", [P, 2, GR * J * R])
        prob = mem.sb("prob", [P, 2, GR * J, R, N])
        prob_t = mem.sb("prob_t", [P, GR, J, P])
        ps_qk = mem.ps("ps_qk", [P, 2, CT])
        ps_v = mem.ps("ps_vv", [P, 512])
        ps_s = mem.ps("ps_ss", [P, R, 512])
        ps_t = mem.ps("ps_pt", [P, J * P])
        ps_o = mem.ps("ps_o", [P, J * P])
        names = ("w_in", "masks", "qkv_mm", "s_mm", "t_mm", "o_mm", "qk_out", "v_out", "t_out", "o_out", "max_done",
                 "sub_done", "exp_done", "sum_done", "inv_done", "norm_done", "vb_clear", "begun")
        (w_in, masks, qkv_mm, s_mm, t_mm, o_mm, qk_out, v_out, t_out, o_out, max_done, sub_done, exp_done, sum_done,
         inv_done, norm_done, vb_clear, begun) = (mem.sem("t_" + n) for n in names)
        scores_view = ps_s[:, :, 0:CT].rearrange("p r (a k) -> p r a k", k=N)
        with nc.Block() as block:

            @block.sync
            def _(sp):
                sp.dma_start(w_qkv[:].rearrange("p k d -> p (k d)"), io["w_qkv"]).then_inc(w_in, 16)

            @block.gpsimd
            def _(pool):
                g = nc.gpsimd
                g.memset(vb[:], 0.0).then_inc(vb_clear, 1)
                c = Chain(pool, masks)
                c.step(g.memset(block_mask[:], 1.0))
                c.step(g.affine_select(out=block_mask[:], in_=block_mask[:], compare_op=ALU.is_ge, fill=0.0, base=0,
                                       pattern=[[-DK, J], [-J * DK, R]], channel_multiplier=1))
                c.step(g.affine_select(out=block_mask[:], in_=block_mask[:], compare_op=ALU.is_ge, fill=0.0,
                                       base=DK - 1, pattern=[[DK, J], [J * DK, R]], channel_multiplier=-1))
                with nc.gpsimd.Fori(0, NC // 2) as i:
                    for k in range(2):
                        pool.wait_ge(inv_done, i * 2 + k + 1)
                        e = prob[:, k].rearrange("p a r n -> p (a r) n")
                        g.tensor_tensor(e, e, total[:, k, :, None].broadcast_to([P, GR * J * R, N]),
                                        ALU.mult).then_inc(norm_done, 1)

            @block.tensor
            def _(pe):
                mm = nc.tensor.matmul

                def project(c):
                    x = xn_t[:, bass.ds(c * CB, CB), :]
                    mm(ps_qk[:, 0, :], w_qkv[:, 0, :], x, start=True, stop=True)
                    mm(ps_qk[:, 1, :], w_qkv[:, 1, :], x, start=True, stop=True)
                    mm(ps_v[:, 0:CT], w_qkv[:, 2, :], x, start=True, stop=True).then_inc(qkv_mm, 1)

                def scores(c):
                    pe.wait_ge(qk_out, c + 1)
                    pe.wait_ge(sub_done, c + 1)
                    pe.sem_inc(begun, 1)
                    for n in range(CB * R):
                            g, q, r = n // 16, (n + n // 4) % 4, n % 4
                            b = g * BG + q
                            rows = slice(32 * r, 32 * r + 32)
                            last = mm(ps_s[32 * q:32 * q + 32, r, g * P:(g + 1) * P], qs[rows, b, :],
                                      km[rows, b].rearrange("p j n -> p (j n)"), start=True, stop=True)
                    last.then_inc(s_mm, 1)

                def turn(c, k):
                    pe.wait_ge(norm_done, c + 1)
                    pe.wait_ge(o_out, c + 1)
                    pe.wait_ge(t_out, c * GR + 2)
                    for g, bank in enumerate((ps_t, ps_o)):
                        for j in range(J):
                            last = nc.tensor.transpose(bank[:, j * P:(j + 1) * P],
                                                       prob[:, k, g * J + j].rearrange("p r n -> p (r n)"), ident[:])
                        last.then_inc(t_mm, 1)

                def mix(c, k):
                    pe.wait_ge(t_out, c * GR + 2 + GR)
                    pe.wait_ge(v_out, c + 1)
                    for b in range(CB):
                        g, q = divmod(b, BG)
                        for j in range(J):
                            last = mm(ps_o[32 * j:32 * j + 32, b * N:(b + 1) * N],
                                      vb[:, k, b, j].rearrange("p r d -> p (r d)"),
                                      prob_t[:, g, j, q * N:(q + 1) * N], start=True, stop=True)
                    last.then_inc(o_mm, 1)

                def body(c, k, before, after):
                    scores(c)
                    if before:
                        turn(c - 1, 1 - k)
                    if after:
                        pe.wait_ge(v_out, c + 1)
                        project(c + 1)
                    if before:
                        mix(c - 1, 1 - k)

                pe.wait_ge(w_in, 16)
                project(0)
                body(0, 0, False, True)
                body(1, 1, True, True)
                with nc.tensor.Fori(1, NC // 2 - 1) as i:
                    body(i * 2, 0, True, True)
                    body(i * 2 + 1, 1, True, True)
                body(NC - 2, 0, True, True)
                body(NC - 1, 1, True, False)
                turn(NC - 1, 1)
                mix(NC - 1, 1)

            @block.scalar
            def _(act):
                fn = nc.scalar.activation
                act.wait_ge(masks, 4)
                fn(warm[:], head_mask[:, 0:1], ACT.Exp)
                act.sem_inc(o_out, 1)
                act.sem_inc(t_out, 2)

                def heads_apart(c):
                    act.wait_ge(qkv_mm, c + 1)
                    nc.scalar.copy(qs[:].rearrange("p b n -> p (b n)"), ps_qk[:, 0, :])
                    for j in range(J):
                        last = fn(km[:, :, j, :], ps_qk[:, 1, :].rearrange("p (b n) -> p b n", n=N), ACT.Copy,
                                  scale=head_mask[:, j:j + 1])
                    last.then_inc(qk_out, 1)

                def turned(c):
                    for g, bank in enumerate((ps_t, ps_o)):
                        act.wait_ge(t_mm, c * GR + g + 1)
                        nc.scalar.copy(prob_t[:, g].rearrange("p j n -> p (j n)"), bank[:]).then_inc(t_out, 1)

                def output(c):
                    act.wait_ge(o_mm, c + 1)
                    nc.scalar.copy(o_t[:, :, bass.ds(c * CB, CB)].rearrange("p n b -> p b n"),
                                   ps_o[:, 0:CT].rearrange("p (b n) -> p b n", n=N)).then_inc(o_out, 1)

                def body(c, k, before, after):
                    act.wait_ge(sub_done, c + 2)
                    e = prob[:, k].rearrange("p a r n -> p (a r n)")
                    fn(e, e, ACT.Exp, scale=SCALE).then_inc(exp_done, 1)
                    if before:
                        turned(c - 1)
                    if after:
                        heads_apart(c + 1)
                    if before:
                        output(c - 1)

                heads_apart(0)
                body(0, 0, False, True)
                body(1, 1, True, True)
                with nc.scalar.Fori(1, NC // 2 - 1) as i:
                    body(i * 2, 0, True, True)
                    body(i * 2 + 1, 1, True, True)
                body(NC - 2, 0, True, True)
                body(NC - 1, 1, True, False)
                turned(NC - 1)
                output(NC - 1)

            @block.vector
            def _(dve):
                v = nc.vector
                dve.wait_ge(masks, 3)
                v.tensor_reduce(head_mask[:], block_mask[:], AX.X, ALU.add).then_inc(masks, 1)
                dve.sem_inc(sub_done, 1)
                dve.wait_ge(vb_clear, 1)

                def place_v(c, k):
                    dve.wait_ge(qkv_mm, c + 1)
                    for r in range(R):
                        rows = slice(32 * r, 32 * r + 32)
                        last = v.transpose(vb[rows, k, :, :, r, :].rearrange("p b j d -> p (b j) d"),
                                           ps_v[rows, 0:CT].rearrange("p (a d) -> p a d", d=DK))
                    last.then_inc(v_out, 1)

                def body(c, k, before, after):
                    dve.wait_ge(s_mm, c + 1)
                    v.tensor_reduce(most[:], scores_view, AX.X, ALU.max).then_inc(max_done, 1)
                    dve.wait_ge(max_done, c + 1)
                    if before:
                        dve.wait_ge(t_mm, (c - 1) * GR)
                    v.tensor_tensor(prob[:, k].rearrange("p a r n -> p r a n"), scores_view,
                                    most[:, :, :, None].broadcast_to([P, R, GR * J, N]), ALU.subtract).then_inc(sub_done, 1)
                    dve.wait_ge(exp_done, c + 1)
                    v.tensor_reduce(total[:, k], prob[:, k].rearrange("p a r n -> p (a r) n"), AX.X,
                                    ALU.add).then_inc(sum_done, 1)
                    dve.wait_ge(sum_done, c + 1)
                    v.reciprocal(total[:, k], total[:, k]).then_inc(inv_done, 1)
                    if after:
                        if before:
                            dve.wait_ge(o_mm, c)
                        place_v(c + 1, 1 - k)

                place_v(0, 0)
                body(0, 0, False, True)
                body(1, 1, False, False)
                dve.wait_ge(o_mm, 1)
                place_v(2, 0)
                with nc.vector.Fori(1, NC // 2 - 1) as i:
                    body(i * 2, 0, True, True)
                    body(i * 2 + 1, 1, True, True)
                body(NC - 2, 0, True, True)
                body(NC - 1, 1, True, False)


E_MOE, HID = 8, 4 * D
TILES = T // P + E_MOE - 1
SLOTS = TILES * P


def project_and_route(nc, io, consts, o_t, x2, xh, slot_i, expert_i, ln2_wb):
    ident, ones = consts[0], consts[4]
    E = E_MOE
    with ExitStack() as ctx:
        mem = Memory(nc, ctx)
        st = NormStats(mem, "ln2")
        w_proj = mem.sb("w_proj", [P, D])
        gate_w = mem.sb("gate_w1", [P, E])
        gate_b = mem.sb("gate_b1", [P, E])
        prefer = mem.sb("prefer1", [P, E])
        before = mem.sb("before", [P, P])
        tile_no = mem.sb("tile_no", [P, TILES])
        restart = mem.sb("restart", [P, E, N])
        xn = mem.sb("xn2", [P, 2, TC * B])
        logits = mem.sb("logits1", [P, N, E])
        top = mem.sb("top1", [P, N])
        eq = mem.sb("eq1", [P, N, E])
        hot = mem.sb("hot1", [P, N, E])
        count = mem.sb("count1", [P, E, N])
        seen = mem.sb("seen1", [P, E, N])
        tiles = mem.sb("tiles1", [P, E])
        tiles_i = mem.sb("tiles_i", [P, E], I32)
        tile_end = mem.sb("tile_end", [P, E])
        first_slot = mem.sb("first_slot", [P, E])
        past = mem.sb("past", [P, TILES, E - 1])
        expert = mem.sb("expert1", [P, TILES])
        ps_p = [mem.ps(f"ps_pr{k}", [P, TC * D]) for k in range(2)]
        ps_x = [mem.ps(f"ps_xt{k}", [P, TC * B]) for k in range(2)]
        ps_l = mem.ps("ps_lg", [P, N, E])
        ps_r = mem.ps("ps_rank", [P, N, E])
        ps_c = mem.ps("ps_count", [P, N, E])
        names = ("w_in", "made", "p_mm", "x2_done", "stats", "own", "rooted", "xh_done", "x_mm", "xn_out", "l_mm",
                 "hot_done", "r_mm")
        w_in, made, p_mm, x2_done, stats, own, rooted, xh_done, x_mm, xn_out, l_mm, hot_done, r_mm = (
            mem.sem("r_" + n) for n in names)
        with nc.Block() as block:

            @block.sync
            def _(sp):
                sp.dma_start(w_proj[:], io["w_proj"]).then_inc(w_in, 16)
                sp.dma_start(gate_w[:], io["gate_w1"]).then_inc(w_in, 16)
                sp.dma_start(gate_b[:], io["gate_b1"].broadcast_to([P, E])).then_inc(w_in, 16)
                sp.dma_start(ln2_wb[:], io["ln2_wb"]).then_inc(w_in, 16)

            @block.gpsimd
            def _(pool):
                g = nc.gpsimd
                c = Chain(pool, made)
                c.step(g.iota(prefer[:], pattern=[[-1, E]], base=E, channel_multiplier=0,
                              allow_small_or_imprecise_dtypes=True))
                c.step(g.iota(tile_no[:], pattern=[[1, TILES]], base=0, channel_multiplier=0,
                              allow_small_or_imprecise_dtypes=True))
                c.step(g.memset(before[:], 1.0))
                c.step(g.affine_select(out=before[:], in_=before[:], compare_op=ALU.is_ge, fill=0.0, base=-1,
                                       pattern=[[1, P]], channel_multiplier=-1))
                c.step(g.memset(restart[:], 1.0))
                c.step(g.memset(restart[:, :, 0], 0.0))

            @block.tensor
            def _(pe):
                mm = nc.tensor.matmul
                pe.wait_ge(w_in, 64)
                for c in range(CHUNKS):
                    if c >= 2:
                        pe.wait_ge(x2_done, c - 1)
                    for k in range(TC):
                        last = mm(ps_p[c % 2][:, k * D:(k + 1) * D], o_t[:, c * TC + k, :], w_proj[:], start=True, stop=True)
                    last.then_inc(p_mm, 1)
                for c in range(CHUNKS + 1):
                    if c < CHUNKS:
                        pe.wait_ge(xh_done, (c + 1) * TC)
                        if c >= 2:
                            pe.wait_ge(xn_out, c - 1)
                        for k in range(TC):
                            last = nc.tensor.transpose(ps_x[c % 2][:, k * B:(k + 1) * B], xh[:, c * TC + k, :], ident[:])
                        last.then_inc(x_mm, 1)
                    if c >= 1:
                        pe.wait_ge(xn_out, c)
                        for k in range(TC):
                            last = mm(ps_l[:, (c - 1) * TC + k, :], xn[:, (c - 1) % 2, k * B:(k + 1) * B], gate_w[:],
                                      start=True, stop=True)
                        last.then_inc(l_mm, 1)
                pe.wait_ge(hot_done, 1)
                pe.wait_ge(made, 6)
                hots = hot[:].rearrange("p t e -> p (t e)")
                mm(ps_r[:].rearrange("p t e -> p (t e)"), before[:], hots, start=True, stop=True).then_inc(r_mm, 1)
                mm(ps_c[:].rearrange("p t e -> p (t e)"), ones[:], hots, start=True, stop=True).then_inc(r_mm, 1)

            @block.scalar
            def _(act):
                act.wait_ge(stats, 1)
                nc.scalar.activation(st.root[:], st.var[:], ACT.Sqrt).then_inc(rooted, 1)
                act.wait_ge(w_in, 64)
                for c in range(CHUNKS):
                    act.wait_ge(x_mm, c + 1)
                    if c >= 2:
                        act.wait_ge(l_mm, c - 1)
                    nc.scalar.activation(xn[:, c % 2, :], ps_x[c % 2][:], ACT.Identity, scale=ln2_wb[:, 0:1],
                                         bias=ln2_wb[:, 1:2]).then_inc(xn_out, 1)

            @block.vector
            def _(dve):
                v = nc.vector
                with nc.vector.Fori(0, CHUNKS // 2) as q:
                    for h in range(2):
                        dve.wait_ge(p_mm, q * 2 + h + 1)
                        here = x2[:, bass.ds((q * 2 + h) * TC, TC), :]
                        v.tensor_tensor(here, ps_p[h][:].rearrange("p (t d) -> p t d", d=D), here, ALU.add).then_inc(x2_done, 1)
                        dve.wait_ge(x2_done, q * 2 + h + 1)
                        for k in range(TC):
                            t = (q * 2 + h) * TC + k
                            last = v.bn_stats(st.six[:, t, :], x2[:, t, :])
                        last.then_inc(own, 1)
                c = Chain(dve, own, CHUNKS)
                dve.wait_ge(own, CHUNKS)
                st.variance(v, c)
                dve.sem_inc(stats, 1)
                dve.wait_ge(rooted, 1)
                st.inverse_root(v, c)
                for t in range(N):
                    v.tensor_scalar(xh[:, t, :], x2[:, t, :], st.mean[:, t:t + 1], st.rstd[:, t:t + 1],
                                    ALU.subtract, ALU.mult).then_inc(xh_done, 1)
                dve.wait_ge(l_mm, CHUNKS)
                dve.wait_ge(made, 6)
                c.step(v.tensor_tensor(logits[:], ps_l[:], gate_b[:, None, :].broadcast_to([P, N, E]), ALU.add))
                c.step(v.tensor_reduce(top[:], logits[:], AX.X, ALU.max))
                c.step(v.tensor_tensor(eq[:], logits[:], top[:, :, None].broadcast_to([P, N, E]), ALU.is_equal))
                c.step(v.tensor_tensor(eq[:], eq[:], prefer[:, None, :].broadcast_to([P, N, E]), ALU.mult))
                c.step(v.tensor_reduce(top[:], eq[:], AX.X, ALU.max))
                v.tensor_tensor(hot[:], eq[:], top[:, :, None].broadcast_to([P, N, E]), ALU.is_equal).then_inc(hot_done, 1)
                dve.wait_ge(r_mm, 2)
                c.step(v.tensor_copy(count[:], ps_c[:].rearrange("p t e -> p e t")))
                c.step(v.tensor_tensor_scan(out=seen[:].rearrange("p e t -> p (e t)"),
                                            data0=restart[:].rearrange("p e t -> p (e t)"),
                                            data1=count[:].rearrange("p e t -> p (e t)"),
                                            initial=0.0, op0=ALU.mult, op1=ALU.add))
                c.step(v.tensor_scalar(tiles_i[:], seen[:, :, N - 1], float(P - 1), None, ALU.add))
                c.step(v.tensor_scalar(tiles_i[:], tiles_i[:], P.bit_length() - 1, None, ALU.logical_shift_right))
                c.step(v.tensor_copy(tiles[:], tiles_i[:]))
                c.step(v.tensor_tensor_scan(out=tile_end[:], data0=ones[:, 0:E], data1=tiles[:], initial=0.0,
                                            op0=ALU.mult, op1=ALU.add))
                c.step(v.tensor_tensor(first_slot[:], tile_end[:], tiles[:], ALU.subtract))
                c.step(v.tensor_scalar(first_slot[:], first_slot[:], float(P), None, ALU.mult))
                c.step(v.tensor_tensor(seen[:], seen[:], count[:], ALU.subtract))
                c.step(v.tensor_tensor(seen[:], seen[:], first_slot[:, :, None].broadcast_to([P, E, N]), ALU.add))
                c.step(v.tensor_tensor(eq[:], ps_r[:], seen[:].rearrange("p e t -> p t e"), ALU.add))
                c.step(v.tensor_tensor(eq[:], eq[:], hot[:], ALU.mult))
                c.step(v.tensor_reduce(top[:], eq[:], AX.X, ALU.add))
                c.step(v.tensor_copy(slot_i[:], top[:]))
                c.step(v.tensor_tensor(past[:], tile_end[:, None, 0:E - 1].broadcast_to([P, TILES, E - 1]),
                                       tile_no[:, :, None].broadcast_to([P, TILES, E - 1]), ALU.is_le))
                c.step(v.tensor_reduce(expert[:], past[:], AX.X, ALU.add))
                c.step(v.tensor_copy(expert_i[:], expert[:]))


def experts(nc, io, consts, x1, x2, xh, slot_i, expert_i, ln2_wb, w1, w2, w_ready, sorted_x, sorted_y, cleared):
    ident = consts[0]
    Q = HID // P
    LEAD = 3
    with ExitStack() as ctx:
        mem = Memory(nc, ctx)
        xt = mem.sb("xt", [P, 2, D])
        x_t = mem.sb("xT", [P, 2, P])
        hid = mem.sb("hid", [P, 2, HID])
        hid_t = mem.sb("hid_t", [P, 2, HID])
        yb = mem.sb("yb", [P, 2, D])
        ps_x = [mem.ps(f"m_x{k}", [P, 512]) for k in range(2)]
        ps_h = [mem.ps(f"m_h{k}", [P, HID]) for k in range(2)]
        ps_t = [mem.ps(f"m_t{k}", [P, HID]) for k in range(2)]
        ps_y = [mem.ps(f"m_y{k}", [P, 512]) for k in range(2)]
        names = ("sent", "loaded0", "loaded1", "x_mm", "x_out", "h_mm", "h_out", "t_mm", "t_out", "y_mm", "y_out", "stored0", "stored1",
                 "fetched", "r_mm", "r_out", "sum", "out")
        (sent, loaded0, loaded1, x_mm, x_out, h_mm, h_out, t_mm, t_out, y_mm, y_out, stored0, stored1, fetched, r_mm, r_out, summed,
         out_done) = (mem.sem("m_" + n) for n in names)
        loaded, stored = (loaded0, loaded1), (stored0, stored1)
        with nc.Block() as block:

            @block.gpsimd
            def _(pool):
                pool.wait_ge(cleared, 16)
                for t in range(N):
                    nc.gpsimd.indirect_dma_start(sorted_x, bass.IndirectOffsetOnAxis(ap=slot_i[:, t:t + 1], axis=0),
                                                 xh[:, t, :], None).then_inc(sent, 16)
                pool.wait_ge(stored0, 16 * ((TILES + 1) // 2) + 16)
                pool.wait_ge(stored1, 16 * (TILES // 2) + 16)
                pool.wait_ge(sent, 16 * N)
                for t in range(N):
                    nc.gpsimd.indirect_dma_start(xh[:, t, :], None, sorted_y,
                                                 bass.IndirectOffsetOnAxis(ap=slot_i[:, t:t + 1], axis=0)).then_inc(fetched, 16)

            @block.sync
            def _(sp):
                sp.wait_ge(sent, 16 * N)

                def load(d, k):
                    sp.wait_ge(x_mm, d + 1)
                    sp.dma_start(xt[:, k, :], sorted_x[bass.ds(d * P, P), :]).then_inc(loaded[k], 16)

                def store(d, k):
                    sp.wait_ge(y_out, d + 3)
                    sp.dma_start(sorted_y[bass.ds(d * P, P), :], yb[:, k, :]).then_inc(stored[k], 16)

                sp.sem_inc(x_mm, 2)
                for d in range(LEAD):
                    load(d, d % 2)
                with nc.sync.Fori(0, (TILES - LEAD) // 2) as i:
                    for k in range(2):
                        load(i * 2 + k + LEAD, (k + LEAD) % 2)
                        store(i * 2 + k, k)
                for d in range(TILES - LEAD, TILES):
                    store(d, d % 2)

            @block.tensor
            def _(pe):
                mm = nc.tensor.matmul
                pe.wait_ge(w_ready, 32)

                def turn(d, k, i):
                    pe.wait_ge(loaded[k], i * 16 + 16)
                    pe.wait_ge(x_out, d + 1)
                    nc.tensor.transpose(ps_x[k][:, 0:P], xt[:, k, :], ident[:]).then_inc(x_mm, 1)

                def up(d, k):
                    e = pe.value_load(expert_i[0:1, bass.ds(d, 1)], min_val=0, max_val=E_MOE - 1)
                    pe.wait_ge(x_out, d + 3)
                    pe.wait_ge(h_out, d + 1)
                    mm(ps_h[k][:], x_t[:, k, :], w1[:, bass.ds(e * HID, HID)], start=True, stop=True).then_inc(h_mm, 1)

                def turn_hidden(d, k):
                    pe.wait_ge(h_out, d + 3)
                    pe.wait_ge(t_out, d + 1)
                    for q in range(Q):
                        last = nc.tensor.transpose(ps_t[k][:, q * P:(q + 1) * P], hid[:, k, q * P:(q + 1) * P], ident[:])
                    last.then_inc(t_mm, 1)

                def down(d, k):
                    e = pe.value_load(expert_i[0:1, bass.ds(d, 1)], min_val=0, max_val=E_MOE - 1)
                    pe.wait_ge(t_out, d + 3)
                    pe.wait_ge(y_out, d + 1)
                    for q in range(Q):
                        last = mm(ps_y[k][:, 0:D], hid_t[:, k, q * P:(q + 1) * P], w2[:, bass.ds(e * (Q * D) + q * D, D)],
                                  start=q == 0, stop=q == Q - 1)
                    last.then_inc(y_mm, 1)

                def body(d, k, i, lo, hi):
                    if hi:
                        turn(d + 1, 1 - k, i + k)
                    up(d, k)
                    if lo:
                        down(d - 1, 1 - k)
                    turn_hidden(d, k)

                turn(0, 0, 0)
                body(0, 0, 0, False, True)
                body(1, 1, 0, True, True)
                with nc.tensor.Fori(1, TILES // 2) as i:
                    body(i * 2, 0, i, True, True)
                    body(i * 2 + 1, 1, i, True, True)
                body(TILES - 1, 0, TILES // 2, True, False)
                down(TILES - 1, 0)
                for c in range(CHUNKS):
                    pe.wait_ge(r_out, c + 1)
                    for k in range(TC):
                        last = nc.tensor.transpose(ps_h[c % 2][:, k * P:(k + 1) * P], x1[:, c * TC + k, :], ident[:])
                    last.then_inc(r_mm, 1)

            @block.scalar
            def _(act):
                fn = nc.scalar.activation
                act.sem_inc(x_out, 2)
                act.sem_inc(h_out, 2)

                def body(d, k):
                    act.wait_ge(x_mm, d + 3)
                    fn(x_t[:, k, :], ps_x[k][:, 0:P], ACT.Identity, scale=ln2_wb[:, 0:1],
                       bias=ln2_wb[:, 1:2]).then_inc(x_out, 1)
                    act.wait_ge(h_mm, d + 1)
                    fn(hid[:, k, :], ps_h[k][:], ACT.Gelu_apprx_tanh).then_inc(h_out, 1)

                body(0, 0)
                body(1, 1)
                with nc.scalar.Fori(1, TILES // 2) as i:
                    for k in range(2):
                        act.wait_ge(t_mm, i * 2 + k - 1)
                        body(i * 2 + k, k)
                act.wait_ge(t_mm, TILES - 2)
                body(TILES - 1, 0)

            @block.vector
            def _(dve):
                v = nc.vector
                dve.sem_inc(t_out, 2)
                dve.sem_inc(y_out, 2)
                dve.sem_inc(r_out, 2)
                for k in range(2):
                    dve.sem_inc(stored[k], 16)

                def body(d, k, i):
                    dve.wait_ge(t_mm, d + 1)
                    v.tensor_copy(hid_t[:, k, :], ps_t[k][:]).then_inc(t_out, 1)
                    dve.wait_ge(y_mm, d + 1)
                    dve.wait_ge(stored[k], i * 16 + 16)
                    v.tensor_copy(yb[:, k, :], ps_y[k][:, 0:D]).then_inc(y_out, 1)

                with nc.vector.Fori(0, TILES // 2) as i:
                    body(i * 2, 0, i)
                    body(i * 2 + 1, 1, i)
                body(TILES - 1, 0, TILES // 2)
                for c in range(CHUNKS):
                    here = x2[:, c * TC:(c + 1) * TC, :]
                    dve.wait_ge(r_mm, c + 1)
                    v.tensor_tensor(here, ps_h[c % 2][:].rearrange("p (t d) -> p t d", d=D), here, ALU.add).then_inc(r_out, 1)
                for c in range(CHUNKS):
                    here = x2[:, c * TC:(c + 1) * TC, :]
                    dve.wait_ge(r_out, c + 3)
                    if c == 0:
                        dve.wait_ge(fetched, 16 * N)
                    v.tensor_tensor(here, here, xh[:, c * TC:(c + 1) * TC, :], ALU.add).then_inc(summed, 1)

        with nc.Block() as block:

            @block.sync
            def _(sp):
                for c in range(CHUNKS):
                    sp.dma_start(io["out"].rearrange("b t d -> b (t d)")[:, c * TC * D:(c + 1) * TC * D],
                                 x2[:, c * TC:(c + 1) * TC, :].rearrange("p t d -> p (t d)")).then_inc(out_done, 16)
                sp.wait_ge(out_done, 16 * CHUNKS)


def adaln_ffn(nc, io):
    with ExitStack() as ctx:
        keep = Memory(nc, ctx)
        buf_a = keep.sb("buf_a", [P, T])
        buf_b = keep.sb("buf_b", [P, T])
        buf_x1 = keep.sb("x1", [P, N, B])
        cw_t = keep.sb("cw_t", [24, T], BF16)
        u_last = keep.sb("u_last", [P, G])
        v_last = keep.sb("v_last", [P, B])
        sorted_x = nc.dram_tensor("sorted_x", (SLOTS, D), F32, kind="Internal").ap()
        sorted_y = nc.dram_tensor("sorted_y", (SLOTS, D), F32, kind="Internal").ap()
        cleared, w_ready = keep.sem("cleared"), keep.sem("w_ready")
        consts = constants(nc, keep, keep)
        sinkhorn(nc, io, consts, buf_a, buf_b, u_last, v_last)
        plan_tokens(nc, io, consts, buf_a, buf_b, u_last, v_last, cw_t)
        routed_ffn(nc, io, buf_b, cw_t, buf_x1)
        zeros = keep.sb("zeros", [P, D])
        xn_t = keep.sb("xn_t", [P, B, N])
        o_t = keep.sb("o_t", [P, N, B])
        w1 = keep.sb("w1", [P, E_MOE * HID])
        w2 = keep.sb("w2", [P, E_MOE * HID])
        slot_i = keep.sb("slot_i", [P, N], I32)
        expert_i = keep.sb("expert_i", [P, TILES], I32)
        ln2_wb = keep.sb("ln2_wb", [P, 2])
        ys = buf_a[:].rearrange("p (t b) -> p t b", b=B)
        rows = buf_a[:].rearrange("p (t d) -> p t d", d=D)
        x2 = buf_b[:].rearrange("p (t d) -> p t d", d=D)
        clear_slots(nc, zeros, sorted_x, cleared, w1, w2, io, w_ready)
        gru(nc, io, buf_x1, ys)
        norm_first(nc, io, consts, ys, x2, xn_t)
        attention(nc, io, consts, xn_t, o_t)
        project_and_route(nc, io, consts, o_t, x2, rows, slot_i, expert_i, ln2_wb)
        experts(nc, io, consts, buf_x1, x2, rows, slot_i, expert_i, ln2_wb, w1, w2, w_ready, sorted_x, sorted_y, cleared)


def clear_slots(nc, zeros, sorted_x, cleared, w1, w2, io, w_ready):
    with ExitStack() as ctx:
        made = Memory(nc, ctx).sem("zeros_made")
        with nc.Block() as block:

            @block.gpsimd
            def _(pool):
                nc.gpsimd.memset(zeros[:], 0.0).then_inc(made, 1)

            @block.sync
            def _(sp):
                sp.dma_start(w1[:], io["w1"]).then_inc(w_ready, 16)
                sp.dma_start(w2[:], io["w2"]).then_inc(w_ready, 16)
                sp.wait_ge(made, 1)
                sp.dma_start(sorted_x.rearrange("(j p) d -> p j d", p=P),
                             zeros[:, None, :].broadcast_to([P, TILES, D])).then_inc(cleared, 16)


def kernel(**inputs):
    import numpy as np
    import concourse.bacc as bacc
    from concourse.bass_utils import run_bass_kernel_spmd as run

    a = {k: np.asarray(v) for k, v in inputs.items()}
    flat = np.ascontiguousarray
    x = a["x"].reshape(T, D)
    wz, wr, wh = (a[f"L1_cond_W{k}"] for k in "zrh")
    laid = {
        "x": x,
        "x_t": x.T,
        "cond_t": a["cond_1024"].T,
        "r_t": a["fside_BxS_0"].reshape(G, P).T,
        "gate_w0_t": a["L0_ffn_gate_weight"].T,
        "gate_b0": a["L0_ffn_gate_bias"].reshape(1, -1),
        "up0_t": np.concatenate([a["L0_ffn_up_weights"].reshape(-1, D), a["L0_ffn_shared_up_weight"]]).T,
        "down0_t": np.concatenate([a["L0_ffn_down_weights"].transpose(0, 2, 1).reshape(-1, D),
                                   a["L0_ffn_shared_down_weight"].T]),
        "gru_wx": np.concatenate([w[:D] for w in (wz, wr, wh)]),
        "gru_wh": np.concatenate([w[D:] for w in (wz, wr, wh)]),
        "gru_wp": a["L1_cond_Wp"],
        "gru_b": np.stack([a[f"L1_cond_b{k}"] for k in "zrhp"], 1),
        "ln1_wb": np.stack([a["L1_ffn_ln1_w"], a["L1_ffn_ln1_b"]], 1),
        "ln2_wb": np.stack([a["L1_ffn_ln2_w"], a["L1_ffn_ln2_b"]], 1),
        "w_qkv": a["L1_ffn_w_qkv"],
        "w_proj": a["L1_ffn_w_proj"].reshape(4, 4, 8, D).transpose(1, 0, 2, 3).reshape(D, D),
        "gate_w1": a["L1_ffn_gate_w"],
        "gate_b1": a["L1_ffn_gate_b"].reshape(1, -1),
        "w1": a["L1_ffn_w1"].transpose(1, 0, 2).reshape(P, -1),
        "w2": a["L1_ffn_w2"].reshape(E_MOE, HID // P, P, D).transpose(2, 0, 1, 3).reshape(P, -1),
    }
    laid = {"in_" + k: flat(v) for k, v in laid.items()}
    nc = bacc.Bacc("TRN2", target_bir_lowering=False, num_devices=1)
    io = {k[3:]: nc.dram_tensor(k, v.shape, F32, kind="ExternalInput").ap() for k, v in laid.items()}
    io["out"] = nc.dram_tensor("out", (B, N, D), F32, kind="ExternalOutput").ap()
    adaln_ffn(nc, io)
    return run(nc, [laid], core_ids=[0]).results[0]["out"]
```
